# Optimizing a Trainium2 kernel written in Bass

```python
import numpy as np
import jax
import jax.numpy as jnp

def _softmax(x, axis=-1):
    return jax.nn.softmax(x, axis=axis)

def _gelu(x):
    return jax.nn.gelu(x, approximate=True)

def _silu(x):
    return jax.nn.silu(x)

def _sigmoid(x):
    return jax.nn.sigmoid(x)

def _layernorm(x, axis=-1, eps=1e-05):
    m = jnp.mean(x, axis=axis, keepdims=True)
    v = jnp.var(x, axis=axis, keepdims=True)
    return (x - m) / jnp.sqrt(v + eps)

def _scatter_add(tgt, idx, src, axis=0):
    return tgt.at[idx].add(src)

def _segment_sum(src, seg, n):
    return jax.ops.segment_sum(src, seg, n)
kernel_name = 'mk_adaln_attn_ffn_d1_seqx_r8_e214e0'

def setup_inputs(seed: int=0):
    np.random.seed(seed)
    _w = jnp.asarray

    def _rec_inputs():
        import jax
        import jax.numpy as jnp
        _rk = jax.random.key(seed)
        x = -0.000125 + 0.9999 * jax.random.normal(jax.random.fold_in(_rk, 1), (8, 128, 512), jnp.float32)
        _lenS = 128 - jax.random.randint(jax.random.fold_in(_rk, 7), (8,), 0, max(1, 128 // 4) + 1, jnp.int32)
        _lenS2 = 128 - jax.random.randint(jax.random.fold_in(_rk, 8), (8,), 0, max(1, 128 // 4) + 1, jnp.int32)
        itok_B_0_7 = jax.random.randint(jax.random.fold_in(_rk, 11), (8,), 0, 8, jnp.int32)
        itok_B_0_23 = jax.random.randint(jax.random.fold_in(_rk, 12), (8,), 0, 24, jnp.int32)
        return (x, itok_B_0_7, itok_B_0_23)
    x, itok_B_0_7, itok_B_0_23 = _rec_inputs()

    def _L0_cond_setup():
        import jax, jax.numpy as jnp
        import numpy as np
        TOP_K = 2
        LANG_BIAS = 5.0
        SCALING = 32.0 / 16.0
        LANGUAGE_PAD_ID = -1
        key = jax.random.key(seed)
        ks = jax.random.split(key, 6)
        B, T, D, O, E, R = (4, 256, 512, 512, 8, 16)
        x = jax.random.normal(ks[0], (B, T, D), dtype=jnp.float32)
        language_ids = jax.random.randint(ks[1], (B,), 0, E).astype(jnp.int64)
        W = jax.random.normal(ks[2], (O, D), dtype=jnp.float32) * (1.0 / np.sqrt(D))
        Wr = jax.random.normal(ks[3], (E, D), dtype=jnp.float32) * (1.0 / np.sqrt(D))
        A = jax.random.normal(ks[4], (E, R, D), dtype=jnp.float32) * (1.0 / np.sqrt(D))
        Bm = jax.random.normal(ks[5], (O, R), dtype=jnp.float32) * 0.0
        Bm = jnp.broadcast_to(Bm, (E, O, R)) + jax.random.normal(ks[5], (E, O, R), dtype=jnp.float32) * 0.02
        return {'x': x, 'language_ids': language_ids, 'W': W, 'Wr': Wr, 'A': A, 'B': Bm}
    _L0_cond_all = _L0_cond_setup()
    _L0_cond_in = {k: v for k, v in _L0_cond_all.items() if k in ('W', 'Wr', 'A', 'B')}
    del _L0_cond_all

    def _L0_attn_setup():
        import jax, jax.numpy as jnp
        import numpy as np
        B, T, H, S, F, G = (2, 256, 512, 128, 1248, 6)
        GRAD_ORDER_MIN = 4
        THD = 2.5
        key = jax.random.key(seed)
        ks = jax.random.split(key, 9)
        sc = 0.02
        hidden_states = jax.random.normal(ks[0], (B, T, H), jnp.float32)
        up_w = jax.random.normal(ks[1], (S, H), jnp.float32) * sc
        gate_w = jax.random.normal(ks[2], (S, H), jnp.float32) / np.sqrt(H)
        local_point = jax.random.normal(ks[3], (S,), jnp.float32)
        local_approx_output = jax.random.normal(ks[4], (H, S), jnp.float32) * sc
        fuse_weight = jax.random.normal(ks[5], (H, S, G), jnp.float32) * sc
        discount_factor = jnp.asarray(np.cumsum(np.log(np.arange(1, G + 1, dtype=np.float64))), jnp.float32)
        ffn_gate_w = jax.random.normal(ks[6], (F, H), jnp.float32) * sc
        ffn_up_w = jax.random.normal(ks[7], (F, H), jnp.float32) * sc
        ffn_down_w = jax.random.normal(ks[8], (H, F), jnp.float32) * sc
        return {'hidden_states': hidden_states, 'up_w': up_w, 'gate_w': gate_w, 'local_point': local_point, 'local_approx_output': local_approx_output, 'fuse_weight': fuse_weight, 'discount_factor': discount_factor, 'ffn_gate_w': ffn_gate_w, 'ffn_up_w': ffn_up_w, 'ffn_down_w': ffn_down_w}
    _L0_attn_all = _L0_attn_setup()
    _L0_attn_in = {k: v for k, v in _L0_attn_all.items() if k in ('up_w', 'gate_w', 'local_point', 'local_approx_output', 'fuse_weight', 'discount_factor', 'ffn_gate_w', 'ffn_up_w', 'ffn_down_w')}
    del _L0_attn_all

    def _L0_cond2_setup():
        import jax, jax.numpy as jnp
        import numpy as np
        R = 16
        ALPHA = 32
        SCALING = ALPHA / R
        SLOTS = 32
        IN_F = 512
        OUT_F = 512
        B, T = (8, 128)
        key = jax.random.key(seed)
        k1, k2, k3, k4, k5, k6 = jax.random.split(key, 6)
        x = jax.random.normal(k1, (B, T, IN_F), dtype=jnp.float32)
        adapter_mapping = jax.random.randint(k2, (B,), 0, SLOTS, dtype=jnp.int32)
        W = jax.random.normal(k3, (OUT_F, IN_F), dtype=jnp.float32) * 0.02
        b = jax.random.normal(k4, (OUT_F,), dtype=jnp.float32) * 0.02
        lora_As = jax.random.normal(k5, (SLOTS, IN_F, R), dtype=jnp.float32) * 0.02
        lora_Bs = jax.random.normal(k6, (SLOTS, R, OUT_F), dtype=jnp.float32) * 0.02
        return {'x': x, 'adapter_mapping': adapter_mapping, 'W': W, 'b': b, 'lora_As': lora_As, 'lora_Bs': lora_Bs}
    _L0_cond2_all = _L0_cond2_setup()
    _L0_cond2_in = {k: v for k, v in _L0_cond2_all.items() if k in ('W', 'b', 'lora_As', 'lora_Bs')}
    del _L0_cond2_all

    def _L0_ffn_setup():
        import jax, jax.numpy as jnp
        import numpy as np
        DIM = 512
        HID = 1376
        R = 16
        SCALING = 32.0 / 16.0

        def _lora_linear(x, w, a, b):
            base = jnp.einsum('bsd,od->bso', x, w)
            low = jnp.einsum('bsr,or->bso', jnp.einsum('bsd,rd->bsr', x, a), b)
            return base + low * SCALING
        key = jax.random.key(seed)
        ks = jax.random.split(key, 10)
        s_in = 1.0 / np.sqrt(DIM)
        s_hid = 1.0 / np.sqrt(HID)
        return {'x': jax.random.normal(ks[0], (4, 256, DIM), jnp.float32), 'w1': jax.random.normal(ks[1], (HID, DIM), jnp.float32) * s_in, 'w3': jax.random.normal(ks[2], (HID, DIM), jnp.float32) * s_in, 'w2': jax.random.normal(ks[3], (DIM, HID), jnp.float32) * s_hid, 'lora_A1': jax.random.normal(ks[4], (R, DIM), jnp.float32) * s_in, 'lora_B1': jax.random.normal(ks[5], (HID, R), jnp.float32) * 0.02, 'lora_A3': jax.random.normal(ks[6], (R, DIM), jnp.float32) * s_in, 'lora_B3': jax.random.normal(ks[7], (HID, R), jnp.float32) * 0.02, 'lora_A2': jax.random.normal(ks[8], (R, HID), jnp.float32) * s_hid, 'lora_B2': jax.random.normal(ks[9], (DIM, R), jnp.float32) * 0.02}
    _L0_ffn_all = _L0_ffn_setup()
    _L0_ffn_in = {k: v for k, v in _L0_ffn_all.items() if k in ('w1', 'w3', 'w2', 'lora_A1', 'lora_B1', 'lora_A3', 'lora_B3', 'lora_A2', 'lora_B2')}
    del _L0_ffn_all
    return {'x': x, 'itok_B_0_7': itok_B_0_7, 'itok_B_0_23': itok_B_0_23, 'L0_cond_W': _L0_cond_in['W'], 'L0_cond_Wr': _L0_cond_in['Wr'], 'L0_cond_A': _L0_cond_in['A'], 'L0_cond_B': _L0_cond_in['B'], 'L0_attn_up_w': _L0_attn_in['up_w'], 'L0_attn_gate_w': _L0_attn_in['gate_w'], 'L0_attn_local_point': _L0_attn_in['local_point'], 'L0_attn_local_approx_output': _L0_attn_in['local_approx_output'], 'L0_attn_fuse_weight': _L0_attn_in['fuse_weight'], 'L0_attn_discount_factor': _L0_attn_in['discount_factor'], 'L0_attn_ffn_gate_w': _L0_attn_in['ffn_gate_w'], 'L0_attn_ffn_up_w': _L0_attn_in['ffn_up_w'], 'L0_attn_ffn_down_w': _L0_attn_in['ffn_down_w'], 'L0_cond2_W': _L0_cond2_in['W'], 'L0_cond2_b': _L0_cond2_in['b'], 'L0_cond2_lora_As': _L0_cond2_in['lora_As'], 'L0_cond2_lora_Bs': _L0_cond2_in['lora_Bs'], 'L0_ffn_w1': _L0_ffn_in['w1'], 'L0_ffn_w3': _L0_ffn_in['w3'], 'L0_ffn_w2': _L0_ffn_in['w2'], 'L0_ffn_lora_A1': _L0_ffn_in['lora_A1'], 'L0_ffn_lora_B1': _L0_ffn_in['lora_B1'], 'L0_ffn_lora_A3': _L0_ffn_in['lora_A3'], 'L0_ffn_lora_B3': _L0_ffn_in['lora_B3'], 'L0_ffn_lora_A2': _L0_ffn_in['lora_A2'], 'L0_ffn_lora_B2': _L0_ffn_in['lora_B2']}

def reference(x, itok_B_0_7, itok_B_0_23, L0_cond_W, L0_cond_Wr, L0_cond_A, L0_cond_B, L0_attn_up_w, L0_attn_gate_w, L0_attn_local_point, L0_attn_local_approx_output, L0_attn_fuse_weight, L0_attn_discount_factor, L0_attn_ffn_gate_w, L0_attn_ffn_up_w, L0_attn_ffn_down_w, L0_cond2_W, L0_cond2_b, L0_cond2_lora_As, L0_cond2_lora_Bs, L0_ffn_w1, L0_ffn_w3, L0_ffn_w2, L0_ffn_lora_A1, L0_ffn_lora_B1, L0_ffn_lora_A3, L0_ffn_lora_B3, L0_ffn_lora_A2, L0_ffn_lora_B2):
    import jax
    import jax.numpy as jnp

    def _L0_cond_ref(x, language_ids, W, Wr, A, B):
        import jax, jax.numpy as jnp
        import numpy as np
        TOP_K = 2
        LANG_BIAS = 5.0
        SCALING = 32.0 / 16.0
        LANGUAGE_PAD_ID = -1
        base = jnp.einsum('btd,od->bto', x, W)
        E = Wr.shape[0]
        logits = jnp.einsum('btd,ed->bte', x.astype(jnp.float32), Wr.astype(jnp.float32))
        expert_targets = language_ids
        valid = expert_targets >= 0
        tgt = jnp.where(valid, expert_targets, 0)
        bias = jax.nn.one_hot(tgt, E, dtype=logits.dtype) * LANG_BIAS
        bias = jnp.where(valid[:, None], bias, 0.0)
        logits = logits + bias[:, None, :]
        topw, topi = jax.lax.top_k(logits, TOP_K)
        weights = jax.nn.softmax(topw, axis=-1)
        gates = jnp.sum(jax.nn.one_hot(topi, E, dtype=weights.dtype) * weights[..., None], axis=-2)
        gates = gates.astype(x.dtype)
        h = jnp.einsum('btd,erd->bter', x, A)
        lora_out = jnp.einsum('bter,bte,eor->bto', h, gates, B)
        return base + SCALING * lora_out

    def _L0_attn_ref(hidden_states, up_w, gate_w, local_point, local_approx_output, fuse_weight, discount_factor, ffn_gate_w, ffn_up_w, ffn_down_w):
        import jax, jax.numpy as jnp
        import numpy as np
        B, T, H, S, F, G = (2, 256, 512, 128, 1248, 6)
        GRAD_ORDER_MIN = 4
        THD = 2.5
        approx_up = hidden_states @ up_w.T
        gate_pre = hidden_states @ gate_w.T
        delta = gate_pre - local_point
        neg_factor = jnp.where(delta > 0, 1.0, -1.0).astype(hidden_states.dtype)
        delta_abs = jnp.abs(delta)
        log_delta = jnp.log(delta_abs)
        keep = (delta_abs <= THD).astype(hidden_states.dtype)
        approx_out = approx_up @ local_approx_output.T
        for idx in range(G):
            m = idx + 1
            dterm = jnp.exp(log_delta * m - discount_factor[idx])
            if m % 2 == 1:
                dterm = dterm * neg_factor
            tmp = dterm * approx_up
            if m > GRAD_ORDER_MIN:
                tmp = tmp * keep
            approx_out = approx_out + tmp @ fuse_weight[:, :, idx].T
        ffn_out = jax.nn.silu(hidden_states @ ffn_gate_w.T) * (hidden_states @ ffn_up_w.T) @ ffn_down_w.T
        return approx_out + ffn_out

    def _L0_cond2_ref(x, adapter_mapping, W, b, lora_As, lora_Bs):
        import jax, jax.numpy as jnp
        import numpy as np
        R = 16
        ALPHA = 32
        SCALING = ALPHA / R
        SLOTS = 32
        IN_F = 512
        OUT_F = 512
        B, T = (8, 128)
        base_out = jnp.einsum('bti,oi->bto', x, W) + b
        A = lora_As[adapter_mapping]
        Bm = lora_Bs[adapter_mapping]
        lora_h = jnp.einsum('bti,bir->btr', x, A)
        lora_out = jnp.einsum('btr,bro->bto', lora_h, Bm)
        return base_out + lora_out * SCALING

    def _L0_ffn_ref(x, w1, w3, w2, lora_A1, lora_B1, lora_A3, lora_B3, lora_A2, lora_B2):
        import jax, jax.numpy as jnp
        import numpy as np
        DIM = 512
        HID = 1376
        R = 16
        SCALING = 32.0 / 16.0

        def _lora_linear(x, w, a, b):
            base = jnp.einsum('bsd,od->bso', x, w)
            low = jnp.einsum('bsr,or->bso', jnp.einsum('bsd,rd->bsr', x, a), b)
            return base + low * SCALING
        h1 = _lora_linear(x, w1, lora_A1, lora_B1)
        h3 = _lora_linear(x, w3, lora_A3, lora_B3)
        g = jax.nn.silu(h1) * h3
        return _lora_linear(g, w2, lora_A2, lora_B2)
    x = x + _L0_attn_ref(_L0_cond_ref(x, itok_B_0_7, L0_cond_W, L0_cond_Wr, L0_cond_A, L0_cond_B), L0_attn_up_w, L0_attn_gate_w, L0_attn_local_point, L0_attn_local_approx_output, L0_attn_fuse_weight, L0_attn_discount_factor, L0_attn_ffn_gate_w, L0_attn_ffn_up_w, L0_attn_ffn_down_w)
    x = x + _L0_ffn_ref(_L0_cond2_ref(x, itok_B_0_23, L0_cond2_W, L0_cond2_b, L0_cond2_lora_As, L0_cond2_lora_Bs), L0_ffn_w1, L0_ffn_w3, L0_ffn_w2, L0_ffn_lora_A1, L0_ffn_lora_B1, L0_ffn_lora_A3, L0_ffn_lora_B3, L0_ffn_lora_A2, L0_ffn_lora_B2)
    return x

_drawn_inputs = setup_inputs


def setup_inputs(seed=0):
    import zlib

    import numpy as np

    out = dict(_drawn_inputs(seed))
    spreads = {}
    factors = {'L0_cond_Wr': 7.215,
     'L0_cond2_b': 8.0,
     'L0_ffn_lora_A1': 2.835,
     'L0_ffn_lora_B1': 2.826,
     'L0_ffn_lora_A3': 2.938,
     'L0_ffn_lora_B3': 2.912,
     'L0_ffn_lora_A2': 2.891,
     'L0_ffn_lora_B2': 2.897}
    for name, (base, spread) in spreads.items():
        noise = np.random.default_rng([zlib.crc32(name.encode()), seed]).standard_normal(out[name].shape)
        drawn = base * np.exp(spread * noise) if base else spread * noise
        out[name] = jnp.asarray(drawn.astype(out[name].dtype))
    for name, factor in factors.items():
        out[name] = (out[name] * factor).astype(out[name].dtype)
    return out
```

```python
from contextlib import ExitStack

import concourse.bass as bass
from concourse import mybir

ALU = mybir.AluOpType
ACT = mybir.ActivationFunctionType
AX = mybir.AxisListType
F32 = mybir.dt.float32
F32R = mybir.dt.float32r
I32 = mybir.dt.int32

P = 128
BATCH, SEQ, D = 8, 128, 512
TOKENS = BATCH * SEQ
HALVES = 2
N = TOKENS // HALVES
TILES = N // P
KC = D // P
EXPERTS, RANK = 8, 16
SLOTS = 32
ORDERS = 6
THD = 2.5
F1, F2 = 1248, 1376
C1, C2 = -(-F1 // P), -(-F2 // P)
SCALING = 2.0
LANG_BIAS = 5.0
BIG = 3.0e38

P_CA = 0
P_CW = 1
P_CB = P_CW + KC
P_UP = P_CB + 1
P_GATE = P_UP + 1
P_AP = P_GATE + 1
P_F1 = P_AP + 1 + ORDERS
P_D1 = P_F1 + 2 * C1
P_W2 = P_D1 + C1
P_F2 = P_W2 + KC
P_D2 = P_F2 + 2 * C2
PIECES = P_D2 + C2
RING = 4

KS = 96
LO_A = slice(64, 96)
LO_B = slice(32, 64)

S_WR = 0
S_LP = S_WR + KC * EXPERTS
S_B2 = S_LP + 1
S_DISC = S_B2 + KC
S_REV = S_DISC + ORDERS
S_IOTA = S_REV + EXPERTS
S_MASK = S_IOTA + EXPERTS
S_ID = S_MASK + BATCH
S_COLS = S_ID + P


def build(nc, x, ids_b, slot_ids, small, pieces, lora_a, lora_b, stk13, stk2, stk_up, out):
    with ExitStack() as ctx:
        def sb(name, shape, dt=F32):
            return ctx.enter_context(nc.sbuf_tensor(name, shape, dt))

        def sem(name):
            return ctx.enter_context(nc.semaphore(name))

        X = sb("X", [P, HALVES, KC, N])
        H = sb("H", [P, HALVES, KC, 2, N], F32R)
        G = sb("G", [P, HALVES, 11, 2, N], F32R)
        WU = sb("WU", [P, 4, 2, N], F32R)
        raw = sb("raw", [P, RING, N])
        T = sb("T", [P, 8, N])
        ga_raw = sb("ga_raw", [P, BATCH * KC * RANK])
        gb_raw = sb("gb_raw", [P, D])
        sm = sb("sm", [P, S_COLS])
        idb = sb("idb", [P, BATCH], I32)
        idf = sb("idf", [P, BATCH])
        slot_i = sb("slot_i", [1, BATCH], I32)
        slot_f = sb("slot_f", [1, 3, BATCH])
        slot_ok = sb("slot_ok", [1, BATCH], I32)
        coef = sb("coef", [P, ORDERS])
        lang = sb("lang", [P, BATCH, EXPERTS])
        S13 = sb("S13", [KS, 2, D], F32R)
        S2 = sb("S2", [KS, C2 * P + D], F32R)
        SU = sb("SU", [KS, 2, 2, P], F32R)
        su_raw = sb("su_raw", [KS, 2, 2, P])
        lg = sb("lg", [P, 2, TILES, EXPERTS])
        lg2 = sb("lg2", [P, 2, TILES, EXPERTS])
        eq = sb("eq", [P, 4, TILES, EXPERTS])
        one1 = sb("one1", [P, 2, TILES, EXPERTS])
        one2 = sb("one2", [P, 2, TILES, EXPERTS])
        col = sb("col", [P, 2, 8, TILES])

        PB = [ctx.enter_context(nc.psum_tensor(f"pb{i}", [P, N], F32)) for i in range(8)]

        XS = 7
        CW = [G[:, 1, k] for k in range(KC)]
        CA, CB, UPW, GATEW = G[:, 1, 4], G[:, 0, 0], G[:, 1, 5], G[:, 1, 6]
        GATED = [G[:, 0, 1], G[:, 0, 2]]
        APW = [WU[:, m] for m in range(4)] + [G[:, 0, XS + m] for m in range(3)]
        W2 = [G[:, 0, k] for k in range(KC)]
        A2S, B2S = G[:, 0, 4], G[:, 0, 5]
        MASKED = [G[:, 1, 0], G[:, 1, 1]]
        DOWN1 = [WU[:, j] for j in range(4)] + [H[:, j // KC, j % KC] for j in range(C1 - 4)]
        DOWN2 = [WU[:, (j + 2) % 4] for j in range(4)] + [H[:, j // KC, j % KC] for j in range(C2 - 4)]

        LOGITS, LOWB, GATEST = (6, 5), (1, 6), (0, 7)
        BASE1 = ((2, 3, 7, 4), (0, 1, 2, 3))
        UPB, GATEB = (4, 6), (5, 7)
        APB = ((0, 1, 2, 3), (4, 5, 6, 7))
        PAIR = ((0, 1), (2, 3))
        DOWNB = ((4, 5, 6, 7), (0, 1, 2, 3))
        LOW2B = (4, 1)
        BASE2 = ((5, 6, 7, 0), (2, 3, 4, 5))
        MERGE = (6, 7)

        x_in = [[sem(f"x_in{h}{c}") for c in range(KC)] for h in range(HALVES)]
        small_in = sem("small_in")
        ids_in = sem("ids_in")
        slots_in = sem("slots_in")
        raw_in = [sem(f"raw_in{s}") for s in range(RING)]
        lora_a_in, lora_b_in = sem("lora_a_in"), sem("lora_b_in")
        stk_in = sem("stk_in")
        su_in = [sem("su_in0"), sem("su_in1")]
        out_done = sem("out_done")
        logits_done = sem("logits_done")
        low_done = sem("low_done")
        gates_t_done = sem("gates_t_done")
        base_done = sem("base_done")
        upgate_done = sem("upgate_done")
        order_done = sem("order_done")
        approx_done = sem("approx_done")
        f1_done, f2_done = sem("f1_done"), sem("f2_done")
        down1_done, down2_done = sem("down1_done"), sem("down2_done")
        merge_done = sem("merge_done")
        hi_w = sem("hi_w")
        hi_x = sem("hi_x")
        hi_low = sem("hi_low")
        hi_base = sem("hi_base")
        hi_term = sem("hi_term")
        hi_g1, hi_g2 = sem("hi_g1"), sem("hi_g2")
        silu1, silu2 = sem("silu1"), sem("silu2")
        hi_x1 = sem("hi_x1")
        hi_lora = sem("hi_lora")
        hi_stk = sem("hi_stk")
        hi_su = sem("hi_su")
        coef_done = sem("coef_done")
        exp_done = sem("exp_done")
        gates_copied = sem("gates_copied")
        abs_done = sem("abs_done")
        lang_done = sem("lang_done")
        slots_ok = sem("slots_ok")
        w_ready = sem("w_ready")
        x_ready = sem("x_ready")
        low_mul = sem("low_mul")
        low_ready = sem("low_ready")
        base_ready = sem("base_ready")
        logits_read = sem("logits_read")
        gap_done = sem("gap_done")
        gates_done = sem("gates_done")
        delta_done = sem("delta_done")
        term_mul = sem("term_mul")
        term_ready = sem("term_ready")
        res_added = sem("res_added")
        g_mul1, g_mul2 = sem("g_mul1"), sem("g_mul2")
        g_ready1, g_ready2 = sem("g_ready1"), sem("g_ready2")
        x1_done = sem("x1_done")
        x1_ready = sem("x1_ready")
        lora_ready = sem("lora_ready")
        stk_ready = sem("stk_ready")
        su_ready = sem("su_ready")
        merged = sem("merged")
        out_ready = sem("out_ready")
        dve_step = sem("dve_step")

        def f32(ap):
            return ap.bitcast(F32)

        def raw_slot(p):
            return raw[:, p % RING, :]

        def raw_count(p):
            return 16 * (p // RING + 1)

        def term_count(h, m):
            return 2 * (m - 1) + h + 1

        block = ctx.enter_context(nc.Block())

        @block.sync
        def _(sp):
            for c in range(KC):
                sp.dma_start(X[:, 0, c, :], x[0, c]).then_inc(x_in[0][c], 16)
                if c < RING:
                    sp.dma_start(raw_slot(c), pieces[c]).then_inc(raw_in[c], 16)
            whole = (PIECES - RING) // RING
            with sp.Fori(0, whole) as i:
                for s in range(RING):
                    sp.wait_ge(w_ready, i * RING + s + 1)
                    sp.dma_start(raw[:, s, :], pieces[i * RING + RING + s]).then_inc(raw_in[s], 16)
            for p in range(RING * (whole + 1), PIECES):
                sp.wait_ge(w_ready, p - RING + 1)
                sp.dma_start(raw_slot(p), pieces[p]).then_inc(raw_in[p % RING], 16)
            for h in range(HALVES):
                for c in range(KC):
                    sp.wait_ge(out_ready, KC * h + c + 1)
                    sp.dma_start(out[h, c], X[:, h, c, :]).then_inc(out_done, 16)
            sp.wait_ge(out_done, 16 * HALVES * KC)

        @block.gpsimd
        def _(pool):
            pool.dma_start(slot_i[:], slot_ids).then_inc(slots_in, 16)
            pool.wait_ge(slots_ok, 1)
            for b in range(BATCH):
                s = pool.value_load(slot_ok[0:1, b:b + 1], min_val=0, max_val=SLOTS - 1)
                pool.dma_start(ga_raw[:, b * KC * RANK:(b + 1) * KC * RANK], lora_a[s]).then_inc(lora_a_in, 16)
                pool.dma_start(gb_raw[b * RANK:(b + 1) * RANK, :], lora_b[s]).then_inc(lora_b_in, 16)
            for c in range(2):
                pool.dma_start(su_raw[:, c], stk_up[c]).then_inc(su_in[c], 16)
            pool.wait_ge(term_ready, 2 * (ORDERS + 1))
            pool.dma_start(T[0:KS, 4:6, :], stk13).then_inc(stk_in, 16)
            pool.wait_ge(stk_ready, 1)
            pool.dma_start(T[0:KS, 4:8, :].rearrange("p a n -> p (a n)")[:, 0:C2 * P + D], stk2).then_inc(stk_in, 16)
            for c in range(2, C2):
                pool.wait_ge(su_ready, c - 1)
                pool.dma_start(su_raw[:, c % 2], stk_up[c]).then_inc(su_in[c % 2], 16)

        @block.scalar
        def _(act):
            act.dma_start(sm[:], small).then_inc(small_in, 16)
            act.dma_start(idb[:], ids_b).then_inc(ids_in, 16)
            for c in range(KC):
                act.dma_start(X[:, 1, c, :], x[1, c]).then_inc(x_in[1][c], 16)

            def copy(o, i):
                return nc.scalar.activation(o, i, ACT.Copy)

            def x_hi(h, c):
                act.wait_ge(x_in[h][c], 16)
                copy(G[:, h, XS + c, 0, :], X[:, h, c, :]).then_inc(hi_x, 1)

            def w_hi(p, dst):
                act.wait_ge(raw_in[p % RING], raw_count(p))
                copy(dst[:, 0, :], raw_slot(p)).then_inc(hi_w, 1)

            def gate_weights(h):
                act.wait_ge(gap_done, h + 1)
                nc.scalar.activation(col[:, h, 5, :], col[:, h, 4, :], ACT.Exp).then_inc(exp_done, 1)

            def gate_low(h):
                act.wait_ge(gates_t_done, h + 1)
                if h == 1:
                    act.wait_ge(low_mul, 1)
                copy(T[:, 1, :], PB[GATEST[h]][:]).then_inc(gates_copied, 1)
                act.wait_ge(low_mul, h + 1)
                copy(GATED[h][:, 0, :], T[:, 2 + h, :]).then_inc(hi_low, 1)

            def base_hi(h, c):
                act.wait_ge(base_done, KC * h + c + 1)
                copy(H[:, h, c, 0, :], PB[BASE1[h][c]][:]).then_inc(hi_base, 1)

            x_hi(0, 0)
            w_hi(P_CA, CA)
            for c in range(1, KC):
                x_hi(0, c)
            w_hi(P_CW, CW[0])
            gate_weights(0)
            for k in range(1, KC):
                w_hi(P_CW + k, CW[k])
            w_hi(P_CB, CB)
            act.wait_ge(small_in, 16)
            nc.scalar.activation(coef[:], sm[:, S_DISC:S_DISC + ORDERS], ACT.Exp, scale=-1.0).then_inc(coef_done, 1)
            for c in range(KC):
                x_hi(1, c)
            gate_low(0)
            w_hi(P_UP, UPW)
            w_hi(P_GATE, GATEW)
            for c in range(KC):
                base_hi(0, c)
            gate_weights(1)
            act.wait_ge(coef_done, 1)
            for m in range(ORDERS + 1):
                p = P_AP + m
                act.wait_ge(raw_in[p % RING], raw_count(p))
                if m >= 4:
                    act.wait_ge(base_done, KC)
                scale = coef[:, m - 1:m] if m else 1.0
                nc.scalar.activation(APW[m][:, 0, :], raw_slot(p), ACT.Copy, scale=scale).then_inc(hi_w, 1)
            gate_low(1)
            for c in range(KC):
                base_hi(1, c)

            def term_hi(h, m):
                if m == 0:
                    act.wait_ge(upgate_done, 2 * h + 1)
                    src = PB[UPB[h]][:]
                else:
                    act.wait_ge(term_mul, term_count(h, m))
                    src = T[:, 4 + 2 * h + m % 2, :]
                copy(G[:, h, m, 0, :], src).then_inc(hi_term, 1)

            for h in range(HALVES):
                term_hi(h, 0)
                act.wait_ge(delta_done, 2 * h + 1)
                nc.scalar.activation(T[:, 2 + h, :], T[:, h, :], ACT.Abs).then_inc(abs_done, 1)
                term_hi(h, 1)
            for m in range(2, ORDERS + 1):
                for h in range(HALVES):
                    term_hi(h, m)

            def ffn_unit(c, h, done, silu, g_mul, hi_g, first):
                act.wait_ge(done, 4 * c + 2 * h + 1)
                if not first:
                    act.wait_ge(g_mul, 2 * c + h - 1)
                nc.scalar.activation(T[:, h, :], PB[PAIR[h][0]][:], ACT.Silu).then_inc(silu, 1)
                act.wait_ge(g_mul, 2 * c + h + 1)
                copy(G[:, h, c, 0, :] if isinstance(c, int) else G[:, h, bass.ds(c, 1), 0, :],
                     T[:, 2 + h, :]).then_inc(hi_g, 1)

            for c in range(2):
                for k in range(2):
                    act.wait_ge(order_done, 2 * c + k + 1)
                    w_hi(P_F1 + 2 * c + k, WU[:, 2 * c + k])

            def ffn1_body(c, par, count):
                for h in range(HALVES):
                    ffn_unit(c, h, f1_done, silu1, g_mul1, hi_g1, False if not isinstance(c, int) else c == 0)
                act.wait_ge(f1_done, 4 * c + 4)
                for k in range(2):
                    s, n = count(k)
                    act.wait_ge(raw_in[s], n)
                    copy(WU[:, 2 * par + k, 0, :], raw[:, s, :]).then_inc(hi_w, 1)

            def static_count(p0):
                return lambda k: ((p0 + k) % RING, raw_count(p0 + k))

            for c in range(2):
                ffn1_body(c, c, static_count(P_F1 + 2 * (c + 2)))
            with act.Fori(0, (C1 - 2) // 2) as i:
                for par in range(2):
                    p0 = P_F1 + 2 * (2 + par + 2)
                    ffn1_body(2 * i + (2 + par), par,
                              lambda k, p0=p0: ((p0 + k) % RING, i * 16 + raw_count(p0 + k)))
            for j in range(4, C1):
                w_hi(P_D1 + j, DOWN1[j])

            act.wait_ge(stk_in, 16)
            copy(S13[:], T[0:KS, 4:6, :]).then_inc(hi_stk, 1)
            act.wait_ge(stk_in, 32)
            stk_flat = T[0:KS, 4:8, :].rearrange("p a n -> p (a n)")[:, 0:C2 * P + D]
            copy(S2[:], stk_flat).then_inc(hi_stk, 1)

            def x1_hi(h):
                act.wait_ge(down1_done, KC * (h + 1))
                for c in range(KC):
                    act.wait_ge(x1_done, KC * h + c + 1)
                    copy(G[:, h, XS + c, 0, :], X[:, h, c, :]).then_inc(hi_x1, 1)

            x1_hi(0)
            act.wait_ge(lora_a_in, 16 * BATCH)
            copy(A2S[:, 0, :].rearrange("p (k b r) -> p k b r", k=KC, b=BATCH),
                 ga_raw[:].rearrange("p (b k r) -> p k b r", k=KC, b=BATCH)).then_inc(hi_lora, 1)
            for k in range(KC):
                w_hi(P_W2 + k, W2[k])
            act.wait_ge(lora_b_in, 16 * BATCH)
            copy(B2S[:, 0, :], gb_raw[:]).then_inc(hi_lora, 1)
            x1_hi(1)

            def su_hi(c, s):
                if s is None:
                    s = c % 2
                act.wait_ge(su_in[s], 16 * (c // 2 + 1) if isinstance(c, int) else c)
                copy(SU[:, s], su_raw[:, s]).then_inc(hi_su, 1)

            for c in range(2):
                su_hi(c, c)

            def low_hi(h):
                act.wait_ge(low_mul, HALVES + h + 1)
                copy(MASKED[h][:, 0, :], T[:, h, :]).then_inc(hi_low, 1)

            def base2_hi(h, c):
                act.wait_ge(base_done, KC * (HALVES + h) + c + 1)
                nc.scalar.activation(H[:, h, c, 0, :], PB[BASE2[h][c]][:], ACT.Identity,
                                     bias=sm[:, S_B2 + c:S_B2 + c + 1]).then_inc(hi_base, 1)

            def merged_hi(c, k):
                p = P_F2 + 2 * c + k
                act.wait_ge(merged, 2 * c + k + 1)
                copy(WU[:, 2 * c + k, 0, :], raw_slot(p)).then_inc(hi_w, 1)

            low_hi(0)
            for c in range(KC):
                base2_hi(0, c)
            low_hi(1)
            for c in range(2):
                for k in range(2):
                    merged_hi(c, k)
            for c in range(KC):
                base2_hi(1, c)

            def ffn2_body(c, par, su_n, raw_k, first):
                if su_n is not None:
                    act.wait_ge(su_in[par], su_n)
                    act.wait_ge(merge_done, 2 * c + 2)
                    copy(SU[:, par], su_raw[:, par]).then_inc(hi_su, 1)
                for h in range(HALVES):
                    ffn_unit(c, h, f2_done, silu2, g_mul2, hi_g2, first)
                act.wait_ge(f2_done, 4 * c + 4)
                for k in range(2):
                    act.wait_ge(merged, 2 * c + 4 + k + 1)
                    copy(WU[:, 2 * par + k, 0, :], raw[:, raw_k(k), :]).then_inc(hi_w, 1)

            def ring2(par):
                return lambda k: (P_F2 + 2 * (par + 2) + k) % RING

            ffn2_body(0, 0, 32, ring2(0), True)
            with act.Fori(0, (C2 - 3) // 2) as i:
                for u in range(2):
                    par = (1 + u) % 2
                    ffn2_body(2 * i + (1 + u), par, i * 16 + 16 * ((3 + u) // 2 + 1), ring2(par), False)
            for c in range(C2 - 2, C2):
                ffn2_body(c, c % 2, None, ring2(c % 2), False)
            for j in range(4, C2):
                act.wait_ge(merged, 2 * C2 + j + 1)
                copy(DOWN2[j][:, 0, :], raw_slot(P_D2 + j)).then_inc(hi_w, 1)

        @block.vector
        def _(dve):
            steps = [0]

            def step(ins):
                steps[0] += 1
                ins.then_inc(dve_step, 1)
                dve.wait_ge(dve_step, steps[0])

            V = nc.vector

            def lo(dst, full, hi):
                return V.tensor_tensor(dst, full, f32(hi), ALU.subtract)

            def x_lo(h, c):
                dve.wait_ge(hi_x, KC * h + c + 1)
                lo(G[:, h, XS + c, 1, :], X[:, h, c, :], G[:, h, XS + c, 0, :]).then_inc(x_ready, 1)

            def w_lo(p, dst):
                dve.wait_ge(hi_w, p + 1)
                lo(dst[:, 1, :], raw_slot(p), dst[:, 0, :]).then_inc(w_ready, 1)

            def small_col(a, n=1):
                return sm[:, a:a + n]

            full4 = [P, TILES, EXPERTS]

            def over_e(ap):
                return ap.unsqueeze(2).to_broadcast(full4)

            rev = small_col(S_REV, EXPERTS).unsqueeze(1).to_broadcast(full4)

            def first_max(h, logits, m, k, one):
                step(V.tensor_reduce(col[:, h, m, :], logits, AX.X, ALU.max))
                step(V.tensor_tensor(eq[:, 2 * h, :, :], logits, over_e(col[:, h, m, :]), ALU.is_equal))
                step(V.tensor_tensor(eq[:, 2 * h + 1, :, :], eq[:, 2 * h, :, :], rev, ALU.mult))
                step(V.tensor_reduce(col[:, h, k, :], eq[:, 2 * h + 1, :, :], AX.X, ALU.max))
                step(V.tensor_tensor(one, rev, over_e(col[:, h, k, :]), ALU.is_equal))

            def route(h):
                dve.wait_ge(logits_done, h + 1)
                ps = PB[LOGITS[h]][:, 0:TILES * EXPERTS].rearrange("p (t e) -> p t e", t=TILES)
                V.scalar_tensor_tensor(lg[:, h], lang[:, TILES * h:TILES * (h + 1), :], LANG_BIAS, ps,
                                       ALU.mult, ALU.add).then_inc(logits_read, 1)
                dve.wait_ge(logits_read, h + 1)
                first_max(h, lg[:, h], 0, 1, one1[:, h])
                step(V.scalar_tensor_tensor(lg2[:, h], one1[:, h], -BIG, lg[:, h], ALU.mult, ALU.add))
                first_max(h, lg2[:, h], 2, 3, one2[:, h])
                V.tensor_tensor(col[:, h, 4, :], col[:, h, 2, :], col[:, h, 0, :], ALU.subtract).then_inc(gap_done, 1)

            def gates(h):
                dve.wait_ge(exp_done, h + 1)
                step(V.tensor_scalar(col[:, h, 6, :], col[:, h, 5, :], 1.0, 1.0 / SCALING, ALU.add, ALU.mult))
                step(V.reciprocal(col[:, h, 6, :], col[:, h, 6, :]))
                step(V.tensor_tensor(col[:, h, 7, :], col[:, h, 5, :], col[:, h, 6, :], ALU.mult))
                step(V.tensor_tensor(one1[:, h], one1[:, h], over_e(col[:, h, 6, :]), ALU.mult))
                step(V.tensor_tensor(one2[:, h], one2[:, h], over_e(col[:, h, 7, :]), ALU.mult))
                step(V.tensor_tensor(one1[:, h], one1[:, h], one2[:, h], ALU.add))
                if h == 1:
                    dve.wait_ge(gates_t_done, 1)
                V.tensor_copy(T[:, 0, :].rearrange("p (a r) -> p a r", r=RANK),
                              one1[:, h].rearrange("p t e -> p (t e)").unsqueeze(2)
                              .to_broadcast([P, TILES * EXPERTS, RANK])).then_inc(gates_done, 1)

            def gate_low(h):
                dve.wait_ge(low_done, h + 1)
                dve.wait_ge(gates_copied, h + 1)
                V.tensor_tensor(T[:, 2 + h, :], PB[LOWB[h]][:], T[:, 1, :], ALU.mult).then_inc(low_mul, 1)
                dve.wait_ge(hi_low, h + 1)
                lo(GATED[h][:, 1, :], T[:, 2 + h, :], GATED[h][:, 0, :]).then_inc(low_ready, 1)

            def base_lo(h, c):
                dve.wait_ge(hi_base, KC * h + c + 1)
                lo(H[:, h, c, 1, :], PB[BASE1[h][c]][:], H[:, h, c, 0, :]).then_inc(base_ready, 1)

            x_lo(0, 0)
            w_lo(P_CA, CA)
            dve.wait_ge(small_in, 16)
            dve.wait_ge(ids_in, 16)
            step(V.tensor_copy(idf[:], idb[:]))
            V.tensor_tensor(lang[:], sm[:, S_IOTA:S_IOTA + EXPERTS].unsqueeze(1).to_broadcast([P, BATCH, EXPERTS]),
                            idf[:].unsqueeze(2).to_broadcast([P, BATCH, EXPERTS]), ALU.is_equal).then_inc(lang_done, 1)
            dve.wait_ge(lang_done, 1)
            for c in range(1, KC):
                x_lo(0, c)
            w_lo(P_CW, CW[0])
            route(0)
            for k in range(1, KC):
                w_lo(P_CW + k, CW[k])
            w_lo(P_CB, CB)
            gates(0)
            for c in range(KC):
                x_lo(1, c)
            gate_low(0)
            dve.wait_ge(slots_in, 16)
            step(V.tensor_copy(slot_f[:, 0, :], slot_i[:]))
            step(V.tensor_scalar(slot_f[:, 1, :], slot_f[:, 0, :], 0.0, float(SLOTS), ALU.is_lt, ALU.mult))
            step(V.tensor_tensor(slot_f[:, 2, :], slot_f[:, 0, :], slot_f[:, 1, :], ALU.add))
            V.tensor_scalar(slot_ok[:], slot_f[:, 2, :], 0.0, SLOTS - 1.0, ALU.max, ALU.min).then_inc(slots_ok, 1)
            w_lo(P_UP, UPW)
            w_lo(P_GATE, GATEW)
            for c in range(KC):
                base_lo(0, c)
            route(1)
            gates(1)
            dve.wait_ge(coef_done, 1)
            for m in range(ORDERS + 1):
                p = P_AP + m
                dve.wait_ge(hi_w, p + 1)
                if m == 0:
                    lo(APW[m][:, 1, :], raw_slot(p), APW[m][:, 0, :]).then_inc(w_ready, 1)
                else:
                    V.scalar_tensor_tensor(APW[m][:, 1, :], raw_slot(p), coef[:, m - 1:m], f32(APW[m][:, 0, :]),
                                           ALU.mult, ALU.subtract).then_inc(w_ready, 1)
            gate_low(1)
            for c in range(KC):
                base_lo(1, c)

            def term(h, m):
                q = T[:, 4 + 2 * h + m % 2, :]
                if m == 1:
                    a, b = PB[UPB[h]][:], T[:, h, :]
                else:
                    a, b = T[:, 4 + 2 * h + (m - 1) % 2, :], T[:, 2 + h if m == 5 else h, :]
                    dve.wait_ge(term_mul, term_count(h, m - 1))
                V.tensor_tensor(q, a, b, ALU.mult).then_inc(term_mul, 1)

            lows = [0]

            def term_lo(h, m):
                lows[0] += 1
                dve.wait_ge(hi_term, lows[0])
                src = T[:, 4 + 2 * h + m % 2, :] if m else PB[UPB[h]][:]
                lo(G[:, h, m, 1, :], src, G[:, h, m, 0, :]).then_inc(term_ready, 1)

            for h in range(HALVES):
                term_lo(h, 0)
                dve.wait_ge(upgate_done, 2 * h + 2)
                V.tensor_scalar(T[:, h, :], PB[GATEB[h]][:], small_col(S_LP), None, ALU.subtract).then_inc(delta_done, 1)
                dve.wait_ge(delta_done, 2 * h + 1)
                term(h, 1)
                dve.wait_ge(abs_done, h + 1)
                V.scalar_tensor_tensor(T[:, 2 + h, :], T[:, 2 + h, :], THD, T[:, h, :], ALU.is_le,
                                       ALU.mult).then_inc(delta_done, 1)
                term_lo(h, 1)
            for m in range(2, ORDERS + 1):
                for h in range(HALVES):
                    if m == 5:
                        dve.wait_ge(delta_done, 2 * h + 2)
                    term(h, m)
                for h in range(HALVES):
                    term_lo(h, m)

            for c in range(2):
                for k in range(2):
                    w_lo(P_F1 + 2 * c + k, WU[:, 2 * c + k])
            for h in range(HALVES):
                for c in range(KC):
                    dve.wait_ge(approx_done, KC * h + c + 1)
                    V.tensor_tensor(X[:, h, c, :], PB[APB[h][c]][:], X[:, h, c, :], ALU.add).then_inc(res_added, 1)

            def ffn_unit(c, h, done, silu, g_mul, hi_g, g_ready):
                dve.wait_ge(done, 4 * c + 2 * h + 2)
                dve.wait_ge(silu, 2 * c + h + 1)
                V.tensor_tensor(T[:, 2 + h, :], PB[PAIR[h][1]][:], T[:, h, :], ALU.mult).then_inc(g_mul, 1)
                dve.wait_ge(hi_g, 2 * c + h + 1)
                g = G[:, h, c, :, :] if isinstance(c, int) else G[:, h, bass.ds(c, 1), :, :].rearrange("p a b n -> p (a b) n")
                lo(g[:, 1, :], T[:, 2 + h, :], g[:, 0, :]).then_inc(g_ready, 1)

            def split_up(n0, par, slot):
                for k in range(2):
                    dve.wait_ge(hi_w, n0 + k)
                    lo(WU[:, 2 * par + k, 1, :], raw[:, slot(k), :], WU[:, 2 * par + k, 0, :]).then_inc(w_ready, 1)

            def ffn1_body(c, par):
                for h in range(HALVES):
                    ffn_unit(c, h, f1_done, silu1, g_mul1, hi_g1, g_ready1)
                split_up(2 * c + (P_F1 + 4 + 1), par, lambda k: (P_F1 + 2 * (par + 2) + k) % RING)

            for c in range(2):
                ffn1_body(c, c)
            with dve.Fori(0, (C1 - 2) // 2) as i:
                for par in range(2):
                    ffn1_body(2 * i + (2 + par), par)
            for j in range(4, C1):
                w_lo(P_D1 + j, DOWN1[j])

            dve.wait_ge(hi_stk, 1)
            V.tensor_tensor(S13[LO_A], T[LO_A, 4:6, :], f32(S13[LO_A]), ALU.subtract).then_inc(stk_ready, 1)
            dve.wait_ge(hi_stk, 2)
            stk_flat = T[0:KS, 4:8, :].rearrange("p a n -> p (a n)")
            V.tensor_tensor(S2[LO_A, 0:C2 * P], stk_flat[LO_A, 0:C2 * P], f32(S2[LO_A, 0:C2 * P]),
                            ALU.subtract).then_inc(stk_ready, 1)
            V.tensor_tensor(S2[LO_B, C2 * P:], stk_flat[LO_B, C2 * P:C2 * P + D], f32(S2[LO_B, C2 * P:]),
                            ALU.subtract).then_inc(stk_ready, 1)

            def x1(h):
                for c in range(KC):
                    dve.wait_ge(down1_done, KC * h + c + 1)
                    dve.wait_ge(res_added, KC * h + c + 1)
                    V.tensor_tensor(X[:, h, c, :], PB[DOWNB[h][c]][:], X[:, h, c, :], ALU.add).then_inc(x1_done, 1)
                for c in range(KC):
                    dve.wait_ge(hi_x1, KC * h + c + 1)
                    lo(G[:, h, XS + c, 1, :], X[:, h, c, :], G[:, h, XS + c, 0, :]).then_inc(x1_ready, 1)

            x1(0)
            dve.wait_ge(hi_lora, 1)
            lo(A2S[:, 1, :].rearrange("p (k b r) -> p k b r", k=KC, b=BATCH),
               ga_raw[:].rearrange("p (b k r) -> p k b r", k=KC, b=BATCH),
               A2S[:, 0, :].rearrange("p (k b r) -> p k b r", k=KC, b=BATCH)).then_inc(lora_ready, 1)
            for k in range(KC):
                w_lo(P_W2 + k, W2[k])
            dve.wait_ge(hi_lora, 2)
            lo(B2S[:, 1, :], gb_raw[:], B2S[:, 0, :]).then_inc(lora_ready, 1)
            x1(1)

            def su_lo(s, n):
                dve.wait_ge(hi_su, n)
                V.tensor_tensor(SU[LO_B, s], su_raw[LO_B, s], f32(SU[LO_B, s]), ALU.subtract).then_inc(su_ready, 1)

            for c in range(2):
                su_lo(c, c + 1)

            def mask_low(h):
                dve.wait_ge(low_done, HALVES + h + 1)
                mask = sm[:, S_MASK + TILES * h:S_MASK + TILES * (h + 1)].unsqueeze(2).to_broadcast([P, TILES, P])
                V.scalar_tensor_tensor(T[:, h, :].rearrange("p (t n) -> p t n", t=TILES),
                                       PB[LOW2B[h]][:].rearrange("p (t n) -> p t n", t=TILES), SCALING, mask,
                                       ALU.mult, ALU.mult).then_inc(low_mul, 1)
                dve.wait_ge(hi_low, HALVES + h + 1)
                lo(MASKED[h][:, 1, :], T[:, h, :], MASKED[h][:, 0, :]).then_inc(low_ready, 1)

            def base2_lo(h, c):
                dve.wait_ge(hi_base, KC * (HALVES + h) + c + 1)
                V.scalar_tensor_tensor(H[:, h, c, 1, :], PB[BASE2[h][c]][:], small_col(S_B2 + c), f32(H[:, h, c, 0, :]),
                                       ALU.add, ALU.subtract).then_inc(base_ready, 1)

            def merge(bank, dst, n):
                dve.wait_ge(merge_done, n)
                V.scalar_tensor_tensor(dst, PB[bank][:], SCALING, dst, ALU.mult, ALU.add).then_inc(merged, 1)

            def merge_up(c):
                for k in range(2):
                    p = P_F2 + 2 * c + k
                    dve.wait_ge(raw_in[p % RING], raw_count(p))
                    merge(MERGE[k], raw_slot(p), 2 * c + k + 1)
                for k in range(2):
                    w_lo(P_F2 + 2 * c + k, WU[:, 2 * c + k])

            mask_low(0)
            for c in range(KC):
                base2_lo(0, c)
            mask_low(1)
            merge_up(0)
            merge_up(1)
            for c in range(KC):
                base2_lo(1, c)

            def ffn2_body(c, par, su, count):
                if su:
                    su_lo(par, c + 3)
                ffn_unit(c, 0, f2_done, silu2, g_mul2, hi_g2, g_ready2)
                for k in range(2):
                    s, n = count(k)
                    dve.wait_ge(raw_in[s], n)
                    merge(MERGE[k], raw[:, s, :], 2 * c + 4 + k + 1)
                ffn_unit(c, 1, f2_done, silu2, g_mul2, hi_g2, g_ready2)
                split_up(2 * c + (P_F2 + 4 + 1), par, lambda k: count(k)[0])

            def static_count(p0):
                return lambda k: ((p0 + k) % RING, raw_count(p0 + k))

            ffn2_body(0, 0, True, static_count(P_F2 + 4))
            with dve.Fori(0, (C2 - 3) // 2) as i:
                for u in range(2):
                    p0 = P_F2 + 2 * (1 + u + 2)
                    ffn2_body(2 * i + (1 + u), (1 + u) % 2, True,
                              lambda k, p0=p0: ((p0 + k) % RING, i * 16 + raw_count(p0 + k)))
            for c in range(C2 - 2, C2):
                ffn2_body(c, c % 2, False, static_count(P_F2 + 2 * (c + 2)))
            for j in range(4, C2):
                p = P_D2 + j
                dve.wait_ge(raw_in[p % RING], raw_count(p))
                merge(j % 2, raw_slot(p), 2 * C2 + j + 1)
                w_lo(p, DOWN2[j])
            for h in range(HALVES):
                for c in range(KC):
                    dve.wait_ge(down2_done, KC * h + c + 1)
                    dve.wait_ge(x1_done, KC * h + c + 1)
                    V.tensor_tensor(X[:, h, c, :], PB[DOWNB[h][c]][:], X[:, h, c, :], ALU.add).then_inc(out_ready, 1)

        @block.tensor
        def _(pe):
            def product(o, w, xx, cols, start, stop):
                pe.matmul(o, w[:, 1, cols], xx[:, 0, :], start=start, stop=False)
                pe.matmul(o, w[:, 0, cols], xx[:, 1, :], start=False, stop=False)
                return pe.matmul(o, w[:, 0, cols], xx[:, 0, :], start=False, stop=stop)

            def chunk(k):
                return slice(k * P, (k + 1) * P)

            def logits(h):
                pe.wait_ge(small_in, 16)
                for c in range(KC):
                    pe.wait_ge(x_in[h][c], 16)
                for t in range(TILES):
                    for k in range(KC):
                        mm = pe.matmul(PB[LOGITS[h]][:, t * EXPERTS:(t + 1) * EXPERTS], X[:, h, k, chunk(t)],
                                       sm[:, S_WR + k * EXPERTS:S_WR + (k + 1) * EXPERTS],
                                       start=(k == 0), stop=(k == KC - 1))
                mm.then_inc(logits_done, 1)

            def low_rank(h, w, bank, ready, n):
                for k in range(KC):
                    pe.wait_ge(ready, n + k + 1)
                    mm = product(PB[bank][:], w, G[:, h, XS + k], chunk(k), k == 0, k == KC - 1)
                mm.then_inc(low_done, 1)

            def base(h, banks, ws, p0, frees):
                for k in range(KC):
                    pe.wait_ge(w_ready, p0 + k + 1)
                    for o in range(KC):
                        if k == 0 and frees[o] is not None:
                            pe.wait_ge(*frees[o])
                        product(PB[banks[o]][:], ws[k], G[:, h, XS + k], chunk(o), k == 0, False)

            def add_low(h, banks, w, low, n):
                pe.wait_ge(low_ready, n)
                for o in range(KC):
                    product(PB[banks[o]][:], w, low, chunk(o), False, True).then_inc(base_done, 1)

            def transpose_gates(h):
                pe.wait_ge(gates_done, h + 1)
                for t in range(TILES):
                    mm = pe.transpose(PB[GATEST[h]][:, chunk(t)], T[:, 0, chunk(t)], sm[:, S_ID:S_ID + P])
                mm.then_inc(gates_t_done, 1)

            logits(0)
            pe.wait_ge(w_ready, P_CA + 1)
            low_rank(0, CA, LOWB[0], x_ready, 0)
            base(0, BASE1[0], CW, P_CW, [None] * KC)
            transpose_gates(0)
            pe.wait_ge(w_ready, P_CB + 1)
            add_low(0, BASE1[0], CB, GATED[0], 1)
            logits(1)
            pe.wait_ge(logits_read, 1)
            low_rank(1, CA, LOWB[1], x_ready, KC)
            base(1, BASE1[1], CW, P_CW, [(gates_copied, 1), (low_mul, 1), (base_ready, 1), (base_ready, 2)])
            pe.wait_ge(base_ready, 3)
            transpose_gates(1)
            add_low(1, BASE1[1], CB, GATED[1], 2)

            frees = {0: (base_ready, 4), 1: (logits_read, 2), 2: (low_mul, 2), 3: (gates_copied, 2)}
            for h in range(HALVES):
                for k in range(2):
                    pe.wait_ge(w_ready, (P_UP, P_GATE)[k] + 1)
                    pe.wait_ge(*frees[2 * h + k])
                    for c in range(KC):
                        pe.wait_ge(base_ready, KC * h + c + 1)
                        mm = product(PB[(UPB, GATEB)[k][h]][:], (UPW, GATEW)[k], H[:, h, c], chunk(c), c == 0, c == KC - 1)
                    mm.then_inc(upgate_done, 1)

            def ready_count(h, m):
                return 2 * h + m + 1 if m < 2 else 2 * m + h + 1

            for m in range(ORDERS + 1):
                pe.wait_ge(w_ready, P_AP + m + 1)
                for h in range(HALVES):
                    pe.wait_ge(term_ready, ready_count(h, m))
                    for o in range(KC):
                        if m == 0 and h == 0:
                            pe.wait_ge(base_ready, KC + o + 1)
                        if m == 0 and h == 1 and o == 0:
                            pe.wait_ge(delta_done, 3)
                            pe.wait_ge(term_mul, 2)
                            pe.wait_ge(term_ready, 3)
                        mm = product(PB[APB[h][o]][:], APW[m], G[:, h, m], chunk(o), m == 0, m == ORDERS)
                        if m == ORDERS:
                            mm.then_inc(approx_done, 1)
                if m < 4:
                    last_order = mm
                    last_order.then_inc(order_done, 1)

            def ffn_unit(c, par, h, done, g_mul, first):
                for k in range(2):
                    if not first:
                        if k == 0:
                            pe.wait_ge(g_mul, 2 * c + h - 1)
                    for d in range(KC):
                        mm = product(PB[PAIR[h][k]][:], WU[:, 2 * par + k], H[:, h, d], chunk(d), d == 0, d == KC - 1)
                    mm.then_inc(done, 1)

            def ffn1_body(c, par, first=False):
                pe.wait_ge(w_ready, 2 * c + (P_F1 + 2))
                for h in range(HALVES):
                    if first:
                        pe.wait_ge(res_added, KC * 0 + 2 * h + 2)
                    ffn_unit(c, par, h, f1_done, g_mul1, first)

            ffn1_body(0, 0, True)
            ffn1_body(1, 1)
            with pe.Fori(0, (C1 - 2) // 2) as i:
                for par in range(2):
                    ffn1_body(2 * i + (2 + par), par)

            def down(h, j, last, slots, p0, done, g_ready, banks):
                pe.wait_ge(w_ready, p0 + j + 1)
                pe.wait_ge(g_ready, 2 * j + h + 1)
                for o in range(KC):
                    mm = product(PB[banks[o]][:], slots[j], G[:, h, j], chunk(o), j == 0, j == last)
                    if j == last:
                        mm.then_inc(done, 1)

            pe.wait_ge(res_added, HALVES * KC)
            for j in range(C1):
                down(0, j, C1 - 1, DOWN1, P_D1, down1_done, g_ready1, DOWNB[0])
            pe.wait_ge(g_mul1, 2 * C1)
            for j in range(C1):
                down(1, j, C1 - 1, DOWN1, P_D1, down1_done, g_ready1, DOWNB[1])

            pe.wait_ge(lora_ready, 1)
            pe.wait_ge(x1_done, 1)
            low_rank(0, A2S, LOW2B[0], x1_ready, 0)
            base(0, BASE2[0], W2, P_W2, [(x1_done, 2), (x1_done, 3), (x1_done, 4), (x1_done, KC + 1)])
            pe.wait_ge(lora_ready, 2)
            add_low(0, BASE2[0], B2S, MASKED[0], HALVES + 1)
            pe.wait_ge(x1_done, KC + 2)
            low_rank(1, A2S, LOW2B[1], x1_ready, KC)

            def merge_up(c, par):
                pe.wait_ge(su_ready, c + 1)
                for k in range(2):
                    if isinstance(c, int) and c == 0:
                        pe.wait_ge(base_ready, HALVES * KC + k + 2)
                    else:
                        pe.wait_ge(merged, 2 * c + k - 1)
                    for d in range(KC):
                        mm = pe.matmul(PB[MERGE[k]][:, chunk(d)], S13[:, k, chunk(d)], SU[:, par, k, :], start=True, stop=True)
                    mm.then_inc(merge_done, 1)

            def merge_down(j, bank):
                pe.matmul(PB[bank][:], S2[:, chunk(j)], S2[:, C2 * P:], start=True, stop=True).then_inc(merge_done, 1)

            pe.wait_ge(stk_ready, 1)
            merge_up(0, 0)
            base(1, BASE2[1], W2, P_W2, [(x1_done, KC + 3), (x1_done, KC + 4), (low_mul, HALVES + 1), (base_ready, 2 * KC + 1)])
            merge_up(1, 1)
            add_low(1, BASE2[1], B2S, MASKED[1], HALVES + 2)

            for c in range(KC):
                pe.wait_ge(base_ready, HALVES * KC + c + 1)

            def ffn2_body(c, par, between, first=False):
                pe.wait_ge(w_ready, 2 * c + (P_F2 + 2))
                if first:
                    pe.wait_ge(low_mul, HALVES + 2)
                ffn_unit(c, par, 0, f2_done, g_mul2, first)
                between()
                if first:
                    pe.wait_ge(base_ready, 2 * HALVES * KC)
                ffn_unit(c, par, 1, f2_done, g_mul2, first)

            ffn2_body(0, 0, lambda: merge_up(2, 0), True)
            with pe.Fori(0, (C2 - 3) // 2) as i:
                for u in range(2):
                    c = 2 * i + (1 + u)
                    ffn2_body(c, (1 + u) % 2, lambda: merge_up(c + 2, (1 + u) % 2))
            pe.wait_ge(stk_ready, 3)
            for n in range(2):
                def merge_first():
                    for k in range(2):
                        pe.wait_ge(merged, 2 * (C2 - 1 + n) + k + 1)
                        merge_down(2 * n + k, MERGE[k])
                ffn2_body(C2 - 2 + n, (C2 - 2 + n) % 2, merge_first)

            def merge_next(j):
                if j < 6:
                    pe.wait_ge(g_mul2, 2 * C2 - 1)
                else:
                    pe.wait_ge(merged, 2 * C2 + j - 1)
                merge_down(j, j % 2)

            merge_next(4)
            merge_next(5)
            pe.wait_ge(merged, 2 * C2 + 4)
            for j in range(C2):
                if 6 <= j + 4 < C2:
                    merge_next(j + 4)
                down(0, j, C2 - 1, DOWN2, P_D2, down2_done, g_ready2, DOWNB[0])
            pe.wait_ge(g_mul2, 2 * C2)
            for j in range(C2):
                down(1, j, C2 - 1, DOWN2, P_D2, down2_done, g_ready2, DOWNB[1])


def kernel(**inputs):
    import numpy as np
    import concourse.bacc as bacc
    from concourse.bass_utils import run_bass_kernel_spmd

    a = {k: np.asarray(v) for k, v in inputs.items()}

    def by_chunk(w):
        return w.T.reshape(-1, P, w.shape[0]).transpose(1, 0, 2)

    def padded(w, rows):
        return np.concatenate([w, np.zeros((rows - w.shape[0],) + w.shape[1:], w.dtype)])

    xs = a["x"].reshape(HALVES, N, KC, P).transpose(0, 2, 3, 1)
    pieces = []
    pieces.append(by_chunk(a["L0_cond_A"].reshape(EXPERTS * RANK, D)).reshape(P, D))
    pieces += list(by_chunk(a["L0_cond_W"]).transpose(1, 0, 2))
    pieces.append(a["L0_cond_B"].transpose(0, 2, 1).reshape(EXPERTS * RANK, D))
    pieces.append(by_chunk(a["L0_attn_up_w"]).reshape(P, D))
    pieces.append(by_chunk(a["L0_attn_gate_w"]).reshape(P, D))
    pieces.append(a["L0_attn_local_approx_output"].T)
    pieces += list(a["L0_attn_fuse_weight"].transpose(2, 1, 0))

    def ffn(gate, up, down, chunks):
        g, u = (by_chunk(padded(w, chunks * P)).reshape(P, KC, chunks, P) for w in (gate, up))
        got = []
        for c in range(chunks):
            got += [g[:, :, c].reshape(P, D), u[:, :, c].reshape(P, D)]
        return got, list(padded(down.T, chunks * P).reshape(chunks, P, D))

    ups1, downs1 = ffn(a["L0_attn_ffn_gate_w"], a["L0_attn_ffn_up_w"], a["L0_attn_ffn_down_w"], C1)
    ups2, downs2 = ffn(a["L0_ffn_w1"], a["L0_ffn_w3"], a["L0_ffn_w2"], C2)
    pieces += ups1 + downs1 + list(by_chunk(a["L0_cond2_W"]).transpose(1, 0, 2)) + ups2 + downs2
    pieces = np.stack(pieces)

    def stacked(w):
        return np.concatenate([padded(w, 32)] * 3)

    b1, b3 = (stacked(padded(a[k], C2 * P).T).reshape(KS, C2, P) for k in ("L0_ffn_lora_B1", "L0_ffn_lora_B3"))
    small = np.concatenate([
        by_chunk(a["L0_cond_Wr"]).reshape(P, KC * EXPERTS),
        a["L0_attn_local_point"].reshape(P, 1),
        a["L0_cond2_b"].reshape(KC, P).T,
        np.broadcast_to(a["L0_attn_discount_factor"], (P, ORDERS)),
        np.broadcast_to((EXPERTS - np.arange(EXPERTS)).astype(np.float32), (P, EXPERTS)),
        np.broadcast_to(np.arange(EXPERTS).astype(np.float32), (P, EXPERTS)),
        np.equal.outer(np.arange(P) // RANK, np.arange(BATCH)).astype(np.float32),
        np.eye(P, dtype=np.float32),
    ], axis=1)
    arrays = {
        "x": xs,
        "ids_b": np.broadcast_to(a["itok_B_0_7"], (P, BATCH)),
        "slot_ids": a["itok_B_0_23"].reshape(1, BATCH),
        "small": small,
        "pieces": pieces,
        "lora_a": a["L0_cond2_lora_As"].reshape(SLOTS, KC, P, RANK).transpose(0, 2, 1, 3).reshape(SLOTS, P, KC * RANK),
        "lora_b": a["L0_cond2_lora_Bs"],
        "stk13": np.stack([stacked(a["L0_ffn_lora_A1"]), stacked(a["L0_ffn_lora_A3"])], axis=1),
        "stk2": np.concatenate([stacked(padded(a["L0_ffn_lora_A2"].T, C2 * P).T), stacked(a["L0_ffn_lora_B2"].T)], axis=1),
        "stk_up": np.stack([b1, b3], axis=2).transpose(1, 0, 2, 3),
    }
    nc = bacc.Bacc("TRN2", target_bir_lowering=False, num_devices=1)
    given, args = {}, []
    for name, v in arrays.items():
        v = np.ascontiguousarray(v)
        given[f"in_{name}"] = v
        args.append(nc.dram_tensor(f"in_{name}", v.shape, mybir.dt.from_np(v.dtype), kind="ExternalInput").ap())
    args.append(nc.dram_tensor("out_x", (HALVES, KC, P, N), F32, kind="ExternalOutput").ap())
    build(nc, *args)
    got = run_bass_kernel_spmd(nc, [given], core_ids=[0]).results[0]["out_x"]
    return got.transpose(0, 3, 1, 2).reshape(BATCH, SEQ, D)
```

```python
from contextlib import ExitStack

import concourse.bass as bass
from concourse import mybir

ALU = mybir.AluOpType
ACT = mybir.ActivationFunctionType
AX = mybir.AxisListType
F32 = mybir.dt.float32
F32R = mybir.dt.float32r
I32 = mybir.dt.int32
BF16 = mybir.dt.bfloat16

P = 128
BATCH, SEQ, D = 8, 128, 512
TOKENS = BATCH * SEQ
HALVES = 2
N = TOKENS // HALVES
TILES = N // P
KC = D // P
EXPERTS, RANK = 8, 16
SLOTS = 32
ORDERS = 6
THD = 2.5
F1, F2 = 1248, 1376
C1, C2 = -(-F1 // P), -(-F2 // P)
SCALING = 2.0
LANG_BIAS = 5.0
BIG = 3.0e38

P_CW = 0
P_CA = P_CW + KC
P_CB = P_CA + 1
P_UP = P_CB + 1
P_GATE = P_UP + 1
P_AP = P_GATE + 1
P_F1 = P_AP + 1 + ORDERS
P_D1 = P_F1 + 2 * C1
P_W2 = P_D1 + C1
P_F2 = P_W2 + KC
P_D2 = P_F2 + 2 * C2
PIECES = P_D2 + C2
WARM = 10
RING = 4

KS = 96
LO_A = slice(64, 96)
LO_B = slice(32, 64)

S_WR = 0
S_LP = S_WR + KC * EXPERTS
S_B2 = S_LP + 1
S_DISC = S_B2 + KC
S_REV = S_DISC + ORDERS
S_IOTA = S_REV + EXPERTS
S_MASK = S_IOTA + EXPERTS
S_ID = S_MASK + BATCH
S_COLS = S_ID + P


def build(nc, x, ids_b, slot_ids, small, pieces, lora_a, lora_b, stk13, stk2, stk_up, out):
    with ExitStack() as ctx:
        def sb(name, shape, dt=F32):
            return ctx.enter_context(nc.sbuf_tensor(name, shape, dt))

        def sem(name):
            return ctx.enter_context(nc.semaphore(name))

        X = sb("X", [P, HALVES, KC, N])
        H = sb("H", [P, HALVES, KC, 2, N], F32R)
        G = sb("G", [P, HALVES, 11, 2, N], F32R)
        WU = sb("WU", [P, 4, 2, N], F32R)
        raw = sb("raw", [P, RING, N])
        T = sb("T", [P, 8, N])
        ga_raw = sb("ga_raw", [P, BATCH * KC * RANK])
        gb_raw = sb("gb_raw", [P, D])
        sm = sb("sm", [P, S_COLS])
        idb = sb("idb", [P, BATCH], I32)
        idf = sb("idf", [P, BATCH])
        slot_i = sb("slot_i", [1, BATCH], I32)
        slot_f = sb("slot_f", [1, 3, BATCH])
        slot_ok = sb("slot_ok", [1, BATCH], I32)
        WR = sb("WR", [P, KC, 2, EXPERTS], F32R)
        warm = sb("warm", [P, N], BF16)
        unused = sb("unused", [P, 1])
        coef = sb("coef", [P, ORDERS])
        lang = sb("lang", [P, BATCH, EXPERTS])
        S13 = sb("S13", [KS, 2, D], F32R)
        S2 = sb("S2", [KS, C2 * P + D], F32R)
        SU = sb("SU", [KS, 2, 2 * P], F32R)
        su_raw = sb("su_raw", [KS, 2, 2 * P])
        lg = sb("lg", [P, 2, TILES, EXPERTS])
        lg2 = sb("lg2", [P, 2, TILES, EXPERTS])
        eq = sb("eq", [P, 4, TILES, EXPERTS])
        one1 = sb("one1", [P, 2, TILES, EXPERTS])
        one2 = sb("one2", [P, 2, TILES, EXPERTS])
        col = sb("col", [P, 2, 8, TILES])

        PS = ctx.enter_context(nc.psum_tensor("PS", [P, 8, N], F32))
        PB = [PS[:, i, :] for i in range(8)]

        XS = 7
        CW = [G[:, 1, k] for k in range(KC)]
        CA, CB, UPW, GATEW = G[:, 1, 4], G[:, 0, 3], G[:, 1, 5], G[:, 1, 6]
        GATED = [G[:, 0, 4], G[:, 0, 5]]
        APW = [WU[:, m] for m in range(4)] + [G[:, 0, XS + m] for m in range(3)]
        W2 = [G[:, 0, k] for k in range(KC)]
        A2S, B2S = G[:, 0, 4], G[:, 0, 5]
        MASKED = [G[:, 1, 0], G[:, 1, 1]]
        DOWN1 = [WU[:, j] for j in range(4)] + [H[:, j // KC, j % KC] for j in range(C1 - 4)]
        DOWN2 = [WU[:, (j + 2) % 4] for j in range(4)] + [H[:, j // KC, j % KC] for j in range(C2 - 4)]

        LOGITS, LOWB, GATEST = (0, 2), (1, 6), (0, 7)
        BASE1 = ((3, 7, 4, 5), (0, 1, 2, 3))
        UPB, GATEB = (4, 6), (5, 7)
        APB = ((0, 1, 2, 3), (4, 5, 6, 7))
        PAIR = ((0, 1), (2, 3))
        DOWNB = ((4, 5, 6, 7), (0, 1, 2, 3))
        LOW2B = (4, 1)
        BASE2 = ((5, 6, 7, 0), (2, 3, 4, 5))
        MERGE = (6, 7)
        MERGE2 = [PS[:, 4 + 2 * k:6 + 2 * k, :].rearrange("p b (a n) -> p (b a) n", a=2) for k in range(2)]

        x_in = [[sem(f"x_in{h}{c}") for c in range(KC)] for h in range(HALVES)]
        small_in = sem("small_in")
        ids_in = sem("ids_in")
        slots_in = sem("slots_in")
        raw_in = [sem(f"raw_in{s}") for s in range(RING)]
        lora_a_in, lora_b_in = sem("lora_a_in"), sem("lora_b_in")
        stk_in = sem("stk_in")
        su_in = sem("su_in")
        out_done = sem("out_done")
        warm_ready = sem("warm_ready")
        logits_done = sem("logits_done")
        low_done = sem("low_done")
        gates_t_done = sem("gates_t_done")
        base_done = sem("base_done")
        upgate_done = sem("upgate_done")
        order_done = sem("order_done")
        approx_done = sem("approx_done")
        f1_done, f2_done = sem("f1_done"), sem("f2_done")
        down1_done, down2_done = sem("down1_done"), sem("down2_done")
        merge_done = sem("merge_done")
        hi_w = sem("hi_w")
        hi_x = sem("hi_x")
        hi_wr = sem("hi_wr")
        hi_low = sem("hi_low")
        hi_base = sem("hi_base")
        hi_term = sem("hi_term")
        hi_g1, hi_g2 = sem("hi_g1"), sem("hi_g2")
        silu1, silu2 = sem("silu1"), sem("silu2")
        hi_x1 = sem("hi_x1")
        hi_lora = sem("hi_lora")
        hi_stk = sem("hi_stk")
        hi_su = sem("hi_su")
        coef_done = sem("coef_done")
        exp_done = sem("exp_done")
        gates_copied = sem("gates_copied")
        abs_done = sem("abs_done")
        wr_ready = sem("wr_ready")
        lang_done = sem("lang_done")
        slots_ok = sem("slots_ok")
        w_ready = sem("w_ready")
        x_ready = sem("x_ready")
        low_mul = sem("low_mul")
        low_ready = sem("low_ready")
        base_ready = sem("base_ready")
        logits_read = sem("logits_read")
        gap_done = sem("gap_done")
        gates_done = sem("gates_done")
        delta_done = sem("delta_done")
        term_mul = sem("term_mul")
        term_ready = sem("term_ready")
        res_added = sem("res_added")
        g_mul1, g_mul2 = sem("g_mul1"), sem("g_mul2")
        g_ready1, g_ready2 = sem("g_ready1"), sem("g_ready2")
        x1_done = sem("x1_done")
        x1_ready = sem("x1_ready")
        lora_ready = sem("lora_ready")
        stk_ready = sem("stk_ready")
        su_ready = sem("su_ready")
        merged = sem("merged")
        out_ready = sem("out_ready")
        dve_step = sem("dve_step")

        def f32(ap):
            return ap.bitcast(F32)

        def raw_slot(p):
            return raw[:, p % RING, :]

        def raw_count(p):
            return 16 * (p // RING + 1)

        def term_count(h, m):
            return 2 * (m - 1) + h + 1

        block = ctx.enter_context(nc.Block())

        @block.sync
        def _(sp):
            for c in range(KC):
                sp.dma_start(X[:, 0, c, :], x[0, c]).then_inc(x_in[0][c], 16)
                if c < RING:
                    sp.dma_start(raw_slot(c), pieces[c]).then_inc(raw_in[c], 16)
            for c in range(KC):
                sp.dma_start(X[:, 1, c, :], x[1, c]).then_inc(x_in[1][c], 16)
            whole = (PIECES - RING) // RING
            with sp.Fori(0, whole) as i:
                for s in range(RING):
                    sp.wait_ge(w_ready, i * RING + s + 1)
                    sp.dma_start(raw[:, s, :], pieces[i * RING + RING + s]).then_inc(raw_in[s], 16)
            for p in range(RING * (whole + 1), PIECES):
                sp.wait_ge(w_ready, p - RING + 1)
                sp.dma_start(raw_slot(p), pieces[p]).then_inc(raw_in[p % RING], 16)
            for h in range(HALVES):
                for c in range(KC):
                    sp.wait_ge(out_ready, KC * h + c + 1)
                    sp.dma_start(out[h, c], X[:, h, c, :]).then_inc(out_done, 16)
            sp.wait_ge(out_done, 16 * HALVES * KC)

        @block.gpsimd
        def _(pool):
            pool.memset(warm[:], 0.0).then_inc(warm_ready, 1)
            pool.dma_start(sm[:], small).then_inc(small_in, 16)
            pool.dma_start(idb[:], ids_b).then_inc(ids_in, 16)
            pool.dma_start(slot_i[:], slot_ids).then_inc(slots_in, 16)
            pool.wait_ge(slots_ok, 1)
            for b in range(BATCH):
                s = pool.value_load(slot_ok[0:1, b:b + 1], min_val=0, max_val=SLOTS - 1)
                pool.dma_start(ga_raw[:, b * KC * RANK:(b + 1) * KC * RANK], lora_a[s]).then_inc(lora_a_in, 16)
                pool.dma_start(gb_raw[b * RANK:(b + 1) * RANK, :], lora_b[s]).then_inc(lora_b_in, 16)
            pool.dma_start(su_raw[:], stk_up[0]).then_inc(su_in, 16)
            pool.wait_ge(term_ready, 2 * (ORDERS + 1))
            pool.dma_start(T[0:KS, 4:6, :], stk13).then_inc(stk_in, 16)
            pool.wait_ge(stk_ready, 1)
            pool.dma_start(T[0:KS, 4:8, :].rearrange("p a n -> p (a n)")[:, 0:C2 * P + D], stk2).then_inc(stk_in, 16)
            for q in range(1, (C2 + 1) // 2):
                pool.wait_ge(su_ready, q)
                pool.dma_start(su_raw[:], stk_up[q]).then_inc(su_in, 16)

        @block.scalar
        def _(act):

            def copy(o, i):
                return nc.scalar.activation(o, i, ACT.Copy)

            def x_hi(h, c):
                act.wait_ge(x_in[h][c], 16)
                copy(G[:, h, XS + c, 0, :], X[:, h, c, :]).then_inc(hi_x, 1)

            def w_hi(p, dst):
                act.wait_ge(raw_in[p % RING], raw_count(p))
                copy(dst[:, 0, :], raw_slot(p)).then_inc(hi_w, 1)

            def gate_weights(h):
                act.wait_ge(gap_done, h + 1)
                nc.scalar.activation(col[:, h, 5, :], col[:, h, 4, :], ACT.Exp).then_inc(exp_done, 1)

            def gate_low(h):
                act.wait_ge(gates_t_done, h + 1)
                if h == 1:
                    act.wait_ge(low_mul, 1)
                copy(T[:, 1, :], PB[GATEST[h]][:]).then_inc(gates_copied, 1)
                act.wait_ge(low_mul, h + 1)
                copy(GATED[h][:, 0, :], T[:, 2 + h, :]).then_inc(hi_low, 1)

            def base_hi(h, c):
                act.wait_ge(base_done, KC * h + c + 1)
                copy(H[:, h, c, 0, :], PB[BASE1[h][c]][:]).then_inc(hi_base, 1)

            act.wait_ge(warm_ready, 1)
            nc.scalar.activation(unused[:], warm[:, 0:1], ACT.Exp)

            for c in range(KC):
                x_hi(0, c)
                w_hi(P_CW + c, CW[c])
            act.wait_ge(small_in, 16)
            nc.scalar.activation(coef[:], sm[:, S_DISC:S_DISC + ORDERS], ACT.Exp, scale=-1.0).then_inc(coef_done, 1)
            copy(WR[:, :, 0, :], sm[:, S_WR:S_WR + KC * EXPERTS].rearrange("p (k e) -> p k e", k=KC)).then_inc(hi_wr, 1)
            w_hi(P_CA, CA)
            for c in range(KC):
                x_hi(1, c)
            w_hi(P_CB, CB)
            gate_weights(0)
            gate_low(0)
            gate_weights(1)
            for c in range(KC):
                base_hi(0, c)
            w_hi(P_UP, UPW)
            w_hi(P_GATE, GATEW)
            act.wait_ge(coef_done, 1)
            for m in range(ORDERS + 1):
                p = P_AP + m
                act.wait_ge(raw_in[p % RING], raw_count(p))
                if m >= 4:
                    act.wait_ge(base_done, KC)
                scale = coef[:, m - 1:m] if m else 1.0
                nc.scalar.activation(APW[m][:, 0, :], raw_slot(p), ACT.Copy, scale=scale).then_inc(hi_w, 1)
            gate_low(1)

            def term_hi(h, m):
                if m == 0:
                    act.wait_ge(upgate_done, 2 * h + 1)
                    src = PB[UPB[h]][:]
                else:
                    act.wait_ge(term_mul, term_count(h, m))
                    src = T[:, 4 + 2 * h + m % 2, :]
                copy(G[:, h, m, 0, :], src).then_inc(hi_term, 1)

            for h in range(HALVES):
                term_hi(h, 0)
                act.wait_ge(delta_done, 2 * h + 1)
                nc.scalar.activation(T[:, 2 + h, :], T[:, h, :], ACT.Abs).then_inc(abs_done, 1)
                term_hi(h, 1)
                if h == 0:
                    for c in range(KC):
                        base_hi(1, c)
            for m in range(2, ORDERS + 1):
                for h in range(HALVES):
                    term_hi(h, m)

            def ffn_unit(c, h, done, silu, g_mul, hi_g, first):
                act.wait_ge(done, 4 * c + 2 * h + 1)
                if not first:
                    act.wait_ge(g_mul, 2 * c + h - 1)
                nc.scalar.activation(T[:, h, :], PB[PAIR[h][0]][:], ACT.Silu).then_inc(silu, 1)
                act.wait_ge(g_mul, 2 * c + h + 1)
                copy(G[:, h, c, 0, :] if isinstance(c, int) else G[:, h, bass.ds(c, 1), 0, :],
                     T[:, 2 + h, :]).then_inc(hi_g, 1)

            for c in range(2):
                for k in range(2):
                    act.wait_ge(order_done, 2 * c + k + 1)
                    w_hi(P_F1 + 2 * c + k, WU[:, 2 * c + k])

            def ffn1_body(c, par, count):
                for h in range(HALVES):
                    ffn_unit(c, h, f1_done, silu1, g_mul1, hi_g1, False if not isinstance(c, int) else c == 0)
                act.wait_ge(f1_done, 4 * c + 4)
                for k in range(2):
                    s, n = count(k)
                    act.wait_ge(raw_in[s], n)
                    copy(WU[:, 2 * par + k, 0, :], raw[:, s, :]).then_inc(hi_w, 1)

            def static_count(p0):
                return lambda k: ((p0 + k) % RING, raw_count(p0 + k))

            for c in range(2):
                ffn1_body(c, c, static_count(P_F1 + 2 * (c + 2)))
            with act.Fori(0, (C1 - 2) // 2) as i:
                for par in range(2):
                    p0 = P_F1 + 2 * (2 + par + 2)
                    ffn1_body(2 * i + (2 + par), par,
                              lambda k, p0=p0: ((p0 + k) % RING, i * 16 + raw_count(p0 + k)))
            for j in range(4, C1):
                w_hi(P_D1 + j, DOWN1[j])

            act.wait_ge(stk_in, 16)
            copy(S13[:], T[0:KS, 4:6, :]).then_inc(hi_stk, 1)
            act.wait_ge(stk_in, 32)
            stk_flat = T[0:KS, 4:8, :].rearrange("p a n -> p (a n)")[:, 0:C2 * P + D]
            copy(S2[:], stk_flat).then_inc(hi_stk, 1)

            def x1_hi(h):
                act.wait_ge(down1_done, KC * (h + 1))
                for c in range(KC):
                    act.wait_ge(x1_done, KC * h + c + 1)
                    copy(G[:, h, XS + c, 0, :], X[:, h, c, :]).then_inc(hi_x1, 1)

            x1_hi(0)
            act.wait_ge(lora_a_in, 16 * BATCH)
            copy(A2S[:, 0, :].rearrange("p (k b r) -> p k b r", k=KC, b=BATCH),
                 ga_raw[:].rearrange("p (b k r) -> p k b r", k=KC, b=BATCH)).then_inc(hi_lora, 1)
            for k in range(KC):
                w_hi(P_W2 + k, W2[k])
            act.wait_ge(lora_b_in, 16 * BATCH)
            copy(B2S[:, 0, :], gb_raw[:]).then_inc(hi_lora, 1)
            x1_hi(1)

            def su_hi(landed):
                act.wait_ge(su_in, landed)
                copy(SU[:], su_raw[:]).then_inc(hi_su, 1)

            su_hi(16)

            def low_hi(h):
                act.wait_ge(low_mul, HALVES + h + 1)
                copy(MASKED[h][:, 0, :], T[:, h, :]).then_inc(hi_low, 1)

            def base2_hi(h, c):
                act.wait_ge(base_done, KC * (HALVES + h) + c + 1)
                nc.scalar.activation(H[:, h, c, 0, :], PB[BASE2[h][c]][:], ACT.Identity,
                                     bias=sm[:, S_B2 + c:S_B2 + c + 1]).then_inc(hi_base, 1)

            def merged_hi(c, par, slot):
                for k in range(2):
                    act.wait_ge(merged, 2 * c + k + 1)
                    copy(WU[:, 2 * par + k, 0, :], raw[:, slot(k), :]).then_inc(hi_w, 1)

            def slot_of(c):
                return lambda k: (P_F2 + 2 * c + k) % RING

            low_hi(0)
            for c in range(KC):
                base2_hi(0, c)
            low_hi(1)
            merged_hi(0, 0, slot_of(0))
            act.wait_ge(merge_done, 2)
            su_hi(32)
            for c in range(KC):
                base2_hi(1, c)

            def unit2(c, h, first=False):
                ffn_unit(c, h, f2_done, silu2, g_mul2, hi_g2, first)

            unit2(0, 0, True)
            merged_hi(1, 1, slot_of(1))
            unit2(0, 1, True)
            act.wait_ge(f2_done, 4)
            merged_hi(2, 0, slot_of(2))
            with act.Fori(0, (C2 - 3) // 2) as i:
                c = 2 * i + 1
                act.wait_ge(merge_done, 2 * i + 4)
                su_hi(i * 16 + 48)
                for u in range(2):
                    for h in range(HALVES):
                        unit2(c + u, h)
                    act.wait_ge(f2_done, 4 * c + (4 * u + 4))
                    merged_hi(c + (u + 2), (1 + u) % 2, slot_of(3 + u))
            for c in range(C2 - 2, C2):
                for h in range(HALVES):
                    unit2(c, h)
                act.wait_ge(f2_done, 4 * c + 4)
                merged_hi(c + 2, c % 2, slot_of(c + 2))
            for j in range(4, C2):
                act.wait_ge(merged, 2 * C2 + j + 1)
                copy(DOWN2[j][:, 0, :], raw_slot(P_D2 + j)).then_inc(hi_w, 1)

        @block.vector
        def _(dve):
            steps = [0]

            def step(ins):
                steps[0] += 1
                ins.then_inc(dve_step, 1)
                dve.wait_ge(dve_step, steps[0])

            V = nc.vector

            def lo(dst, full, hi):
                return V.tensor_tensor(dst, full, f32(hi), ALU.subtract)

            def x_lo(h, c):
                dve.wait_ge(hi_x, KC * h + c + 1)
                lo(G[:, h, XS + c, 1, :], X[:, h, c, :], G[:, h, XS + c, 0, :]).then_inc(x_ready, 1)

            def w_lo(p, dst):
                dve.wait_ge(hi_w, p + 1)
                lo(dst[:, 1, :], raw_slot(p), dst[:, 0, :]).then_inc(w_ready, 1)

            def small_col(a, n=1):
                return sm[:, a:a + n]

            full4 = [P, TILES, EXPERTS]

            def over_e(ap):
                return ap.unsqueeze(2).to_broadcast(full4)

            rev = small_col(S_REV, EXPERTS).unsqueeze(1).to_broadcast(full4)

            def first_max(h, logits, m, k, one):
                step(V.tensor_reduce(col[:, h, m, :], logits, AX.X, ALU.max))
                step(V.tensor_tensor(eq[:, 2 * h, :, :], logits, over_e(col[:, h, m, :]), ALU.is_equal))
                step(V.tensor_tensor(eq[:, 2 * h + 1, :, :], eq[:, 2 * h, :, :], rev, ALU.mult))
                step(V.tensor_reduce(col[:, h, k, :], eq[:, 2 * h + 1, :, :], AX.X, ALU.max))
                step(V.tensor_tensor(one, rev, over_e(col[:, h, k, :]), ALU.is_equal))

            def route(h):
                dve.wait_ge(logits_done, h + 1)
                ps = PB[LOGITS[h]][:, 0:TILES * 2 * EXPERTS].rearrange("p (t a e) -> p t a e", t=TILES, a=2)
                step(V.scalar_tensor_tensor(lg2[:, h], lang[:, TILES * h:TILES * (h + 1), :], LANG_BIAS, ps[:, :, 0, :],
                                            ALU.mult, ALU.add))
                V.tensor_tensor(lg[:, h], ps[:, :, 1, :], lg2[:, h], ALU.add).then_inc(logits_read, 1)
                dve.wait_ge(logits_read, h + 1)
                first_max(h, lg[:, h], 0, 1, one1[:, h])
                step(V.scalar_tensor_tensor(lg2[:, h], one1[:, h], -BIG, lg[:, h], ALU.mult, ALU.add))
                first_max(h, lg2[:, h], 2, 3, one2[:, h])
                V.tensor_tensor(col[:, h, 4, :], col[:, h, 2, :], col[:, h, 0, :], ALU.subtract).then_inc(gap_done, 1)

            def gates(h):
                dve.wait_ge(exp_done, h + 1)
                step(V.tensor_scalar(col[:, h, 6, :], col[:, h, 5, :], 1.0, 1.0 / SCALING, ALU.add, ALU.mult))
                step(V.reciprocal(col[:, h, 6, :], col[:, h, 6, :]))
                step(V.tensor_tensor(col[:, h, 7, :], col[:, h, 5, :], col[:, h, 6, :], ALU.mult))
                step(V.tensor_tensor(one1[:, h], one1[:, h], over_e(col[:, h, 6, :]), ALU.mult))
                step(V.tensor_tensor(one2[:, h], one2[:, h], over_e(col[:, h, 7, :]), ALU.mult))
                step(V.tensor_tensor(one1[:, h], one1[:, h], one2[:, h], ALU.add))
                if h == 1:
                    dve.wait_ge(gates_t_done, 1)
                V.tensor_copy(T[:, 0, :].rearrange("p (a r) -> p a r", r=RANK),
                              one1[:, h].rearrange("p t e -> p (t e)").unsqueeze(2)
                              .to_broadcast([P, TILES * EXPERTS, RANK])).then_inc(gates_done, 1)

            def gate_low(h):
                dve.wait_ge(low_done, h + 1)
                dve.wait_ge(gates_copied, h + 1)
                V.tensor_tensor(T[:, 2 + h, :], PB[LOWB[h]][:], T[:, 1, :], ALU.mult).then_inc(low_mul, 1)
                dve.wait_ge(hi_low, h + 1)
                lo(GATED[h][:, 1, :], T[:, 2 + h, :], GATED[h][:, 0, :]).then_inc(low_ready, 1)

            def base_lo(h, c):
                dve.wait_ge(hi_base, KC * h + c + 1)
                lo(H[:, h, c, 1, :], PB[BASE1[h][c]][:], H[:, h, c, 0, :]).then_inc(base_ready, 1)

            for c in range(KC):
                x_lo(0, c)
                w_lo(P_CW + c, CW[c])
            dve.wait_ge(small_in, 16)
            dve.wait_ge(hi_wr, 1)
            lo(WR[:, :, 1, :], sm[:, S_WR:S_WR + KC * EXPERTS].rearrange("p (k e) -> p k e", k=KC),
               WR[:, :, 0, :]).then_inc(wr_ready, 1)
            dve.wait_ge(ids_in, 16)
            step(V.tensor_copy(idf[:], idb[:]))
            V.tensor_tensor(lang[:], sm[:, S_IOTA:S_IOTA + EXPERTS].unsqueeze(1).to_broadcast([P, BATCH, EXPERTS]),
                            idf[:].unsqueeze(2).to_broadcast([P, BATCH, EXPERTS]), ALU.is_equal).then_inc(lang_done, 1)
            dve.wait_ge(lang_done, 1)
            w_lo(P_CA, CA)
            for c in range(KC):
                x_lo(1, c)
            w_lo(P_CB, CB)
            route(0)
            gates(0)
            gate_low(0)
            route(1)
            for c in range(KC):
                base_lo(0, c)
            gates(1)
            dve.wait_ge(slots_in, 16)
            step(V.tensor_copy(slot_f[:, 0, :], slot_i[:]))
            step(V.tensor_scalar(slot_f[:, 1, :], slot_f[:, 0, :], 0.0, float(SLOTS), ALU.is_lt, ALU.mult))
            step(V.tensor_tensor(slot_f[:, 2, :], slot_f[:, 0, :], slot_f[:, 1, :], ALU.add))
            V.tensor_scalar(slot_ok[:], slot_f[:, 2, :], 0.0, SLOTS - 1.0, ALU.max, ALU.min).then_inc(slots_ok, 1)
            w_lo(P_UP, UPW)
            w_lo(P_GATE, GATEW)
            dve.wait_ge(coef_done, 1)
            for m in range(ORDERS + 1):
                p = P_AP + m
                dve.wait_ge(hi_w, p + 1)
                if m == 0:
                    lo(APW[m][:, 1, :], raw_slot(p), APW[m][:, 0, :]).then_inc(w_ready, 1)
                else:
                    V.scalar_tensor_tensor(APW[m][:, 1, :], raw_slot(p), coef[:, m - 1:m], f32(APW[m][:, 0, :]),
                                           ALU.mult, ALU.subtract).then_inc(w_ready, 1)
            gate_low(1)

            def term(h, m):
                q = T[:, 4 + 2 * h + m % 2, :]
                if m == 1:
                    a, b = PB[UPB[h]][:], T[:, h, :]
                else:
                    a, b = T[:, 4 + 2 * h + (m - 1) % 2, :], T[:, 2 + h if m == 5 else h, :]
                    dve.wait_ge(term_mul, term_count(h, m - 1))
                V.tensor_tensor(q, a, b, ALU.mult).then_inc(term_mul, 1)

            lows = [0]

            def term_lo(h, m):
                lows[0] += 1
                dve.wait_ge(hi_term, lows[0])
                src = T[:, 4 + 2 * h + m % 2, :] if m else PB[UPB[h]][:]
                lo(G[:, h, m, 1, :], src, G[:, h, m, 0, :]).then_inc(term_ready, 1)

            for h in range(HALVES):
                term_lo(h, 0)
                dve.wait_ge(upgate_done, 2 * h + 2)
                V.tensor_scalar(T[:, h, :], PB[GATEB[h]][:], small_col(S_LP), None, ALU.subtract).then_inc(delta_done, 1)
                dve.wait_ge(delta_done, 2 * h + 1)
                term(h, 1)
                if h == 0:
                    for c in range(KC):
                        base_lo(1, c)
                dve.wait_ge(abs_done, h + 1)
                V.scalar_tensor_tensor(T[:, 2 + h, :], T[:, 2 + h, :], THD, T[:, h, :], ALU.is_le,
                                       ALU.mult).then_inc(delta_done, 1)
                term_lo(h, 1)
            for m in range(2, ORDERS + 1):
                for h in range(HALVES):
                    if m == 5:
                        dve.wait_ge(delta_done, 2 * h + 2)
                    term(h, m)
                for h in range(HALVES):
                    term_lo(h, m)

            for c in range(2):
                for k in range(2):
                    w_lo(P_F1 + 2 * c + k, WU[:, 2 * c + k])
            for h in range(HALVES):
                for c in range(KC):
                    dve.wait_ge(approx_done, KC * h + c + 1)
                    V.tensor_tensor(X[:, h, c, :], PB[APB[h][c]][:], X[:, h, c, :], ALU.add).then_inc(res_added, 1)

            def ffn_unit(c, h, done, silu, g_mul, hi_g, g_ready):
                dve.wait_ge(done, 4 * c + 2 * h + 2)
                dve.wait_ge(silu, 2 * c + h + 1)
                V.tensor_tensor(T[:, 2 + h, :], PB[PAIR[h][1]][:], T[:, h, :], ALU.mult).then_inc(g_mul, 1)
                dve.wait_ge(hi_g, 2 * c + h + 1)
                g = G[:, h, c, :, :] if isinstance(c, int) else G[:, h, bass.ds(c, 1), :, :].rearrange("p a b n -> p (a b) n")
                lo(g[:, 1, :], T[:, 2 + h, :], g[:, 0, :]).then_inc(g_ready, 1)

            def split_up(n0, par, slot):
                for k in range(2):
                    dve.wait_ge(hi_w, n0 + k)
                    lo(WU[:, 2 * par + k, 1, :], raw[:, slot(k), :], WU[:, 2 * par + k, 0, :]).then_inc(w_ready, 1)

            def ffn1_body(c, par):
                for h in range(HALVES):
                    ffn_unit(c, h, f1_done, silu1, g_mul1, hi_g1, g_ready1)
                split_up(2 * c + (P_F1 + 4 + 1), par, lambda k: (P_F1 + 2 * (par + 2) + k) % RING)

            for c in range(2):
                ffn1_body(c, c)
            with dve.Fori(0, (C1 - 2) // 2) as i:
                for par in range(2):
                    ffn1_body(2 * i + (2 + par), par)
            for j in range(4, C1):
                w_lo(P_D1 + j, DOWN1[j])

            dve.wait_ge(hi_stk, 1)
            V.tensor_tensor(S13[LO_A], T[LO_A, 4:6, :], f32(S13[LO_A]), ALU.subtract).then_inc(stk_ready, 1)
            dve.wait_ge(hi_stk, 2)
            stk_flat = T[0:KS, 4:8, :].rearrange("p a n -> p (a n)")
            V.tensor_tensor(S2[LO_A, 0:C2 * P], stk_flat[LO_A, 0:C2 * P], f32(S2[LO_A, 0:C2 * P]),
                            ALU.subtract).then_inc(stk_ready, 1)
            V.tensor_tensor(S2[LO_B, C2 * P:], stk_flat[LO_B, C2 * P:C2 * P + D], f32(S2[LO_B, C2 * P:]),
                            ALU.subtract).then_inc(stk_ready, 1)

            def x1(h):
                for c in range(KC):
                    dve.wait_ge(down1_done, KC * h + c + 1)
                    dve.wait_ge(res_added, KC * h + c + 1)
                    V.tensor_tensor(X[:, h, c, :], PB[DOWNB[h][c]][:], X[:, h, c, :], ALU.add).then_inc(x1_done, 1)
                for c in range(KC):
                    dve.wait_ge(hi_x1, KC * h + c + 1)
                    lo(G[:, h, XS + c, 1, :], X[:, h, c, :], G[:, h, XS + c, 0, :]).then_inc(x1_ready, 1)

            x1(0)
            dve.wait_ge(hi_lora, 1)
            lo(A2S[:, 1, :].rearrange("p (k b r) -> p k b r", k=KC, b=BATCH),
               ga_raw[:].rearrange("p (b k r) -> p k b r", k=KC, b=BATCH),
               A2S[:, 0, :].rearrange("p (k b r) -> p k b r", k=KC, b=BATCH)).then_inc(lora_ready, 1)
            for k in range(KC):
                w_lo(P_W2 + k, W2[k])
            dve.wait_ge(hi_lora, 2)
            lo(B2S[:, 1, :], gb_raw[:], B2S[:, 0, :]).then_inc(lora_ready, 1)
            x1(1)

            def su_lo(n):
                dve.wait_ge(hi_su, n)
                V.tensor_tensor(SU[LO_B], su_raw[LO_B], f32(SU[LO_B]), ALU.subtract).then_inc(su_ready, 1)

            su_lo(1)

            def mask_low(h):
                dve.wait_ge(low_done, HALVES + h + 1)
                mask = sm[:, S_MASK + TILES * h:S_MASK + TILES * (h + 1)].unsqueeze(2).to_broadcast([P, TILES, P])
                V.scalar_tensor_tensor(T[:, h, :].rearrange("p (t n) -> p t n", t=TILES),
                                       PB[LOW2B[h]][:].rearrange("p (t n) -> p t n", t=TILES), SCALING, mask,
                                       ALU.mult, ALU.mult).then_inc(low_mul, 1)
                dve.wait_ge(hi_low, HALVES + h + 1)
                lo(MASKED[h][:, 1, :], T[:, h, :], MASKED[h][:, 0, :]).then_inc(low_ready, 1)

            def base2_lo(h, c):
                dve.wait_ge(hi_base, KC * (HALVES + h) + c + 1)
                V.scalar_tensor_tensor(H[:, h, c, 1, :], PB[BASE2[h][c]][:], small_col(S_B2 + c), f32(H[:, h, c, 0, :]),
                                       ALU.add, ALU.subtract).then_inc(base_ready, 1)

            def merge(update, dst, n):
                dve.wait_ge(merge_done, n)
                V.scalar_tensor_tensor(dst, update, SCALING, dst, ALU.mult, ALU.add).then_inc(merged, 1)

            def landed(c):
                p0 = P_F2 + 2 * c
                return lambda k: ((p0 + k) % RING, raw_count(p0 + k))

            def merge_pair(n0, which, count):
                for k in range(2):
                    s, n = count(k)
                    dve.wait_ge(raw_in[s], n)
                    merge(MERGE2[k][:, :, which * P:(which + 1) * P],
                          raw[:, s, :].rearrange("p (d n) -> p d n", d=KC), n0 + k)

            def merge_one(n0, count):
                for k in range(2):
                    s, n = count(k)
                    dve.wait_ge(raw_in[s], n)
                    merge(PB[MERGE[k]], raw[:, s, :], n0 + k)

            mask_low(0)
            for c in range(KC):
                base2_lo(0, c)
            mask_low(1)
            merge_one(1, landed(0))
            split_up(P_F2 + 1, 0, lambda k: landed(0)(k)[0])
            su_lo(2)
            for c in range(KC):
                base2_lo(1, c)

            def unit2(c, h):
                ffn_unit(c, h, f2_done, silu2, g_mul2, hi_g2, g_ready2)

            unit2(0, 0)
            merge_pair(3, 0, landed(1))
            split_up(P_F2 + 3, 1, lambda k: landed(1)(k)[0])
            unit2(0, 1)
            merge_pair(3, 1, landed(2))
            split_up(P_F2 + 5, 0, lambda k: landed(2)(k)[0])
            with dve.Fori(0, (C2 - 3) // 2) as i:
                c = 2 * i + 1
                su_lo(i + 3)
                for u in range(2):
                    def count(k, at=landed(3 + u)):
                        return at(k)[0], i * 16 + at(k)[1]
                    unit2(c + u, 0)
                    merge_pair(2 * i + 5, u, count)
                    unit2(c + u, 1)
                    split_up(4 * i + (P_F2 + 6 + 2 * u + 1), (1 + u) % 2, lambda k: count(k)[0])
            for c in range(C2 - 2, C2):
                unit2(c, 0)
                merge_one(C2 + 2 + 2 * (c - C2 + 2), landed(c + 2))
                unit2(c, 1)
                split_up(P_F2 + 2 * (c + 2) + 1, c % 2, lambda k: landed(c + 2)(k)[0])
            for j in range(4, C2):
                p = P_D2 + j
                dve.wait_ge(raw_in[p % RING], raw_count(p))
                merge(PB[j % 2], raw_slot(p), C2 + 1 + j + 1)
                w_lo(p, DOWN2[j])
            for h in range(HALVES):
                for c in range(KC):
                    dve.wait_ge(down2_done, KC * h + c + 1)
                    dve.wait_ge(x1_done, KC * h + c + 1)
                    V.tensor_tensor(X[:, h, c, :], PB[DOWNB[h][c]][:], X[:, h, c, :], ALU.add).then_inc(out_ready, 1)

        @block.tensor
        def _(pe):
            def product(o, w, xx, cols, start, stop):
                pe.matmul(o, w[:, 1, cols], xx[:, 0, :], start=start, stop=False)
                pe.matmul(o, w[:, 0, cols], xx[:, 1, :], start=False, stop=False)
                return pe.matmul(o, w[:, 0, cols], xx[:, 0, :], start=False, stop=stop)

            def chunk(k):
                return slice(k * P, (k + 1) * P)

            def logits(h):
                pe.wait_ge(wr_ready, 1)
                pe.wait_ge(x_ready, KC * (h + 1))
                for t in range(TILES):
                    o = PB[LOGITS[h]][:, t * 2 * EXPERTS:(t + 1) * 2 * EXPERTS]
                    for k in range(KC):
                        xk = G[:, h, XS + k]
                        if k:
                            pe.matmul(o[:, 0:EXPERTS], xk[:, 1, chunk(t)], WR[:, k, 0, :],
                                      start=False, stop=False, skip_group_check=True)
                        mm = pe.matmul(o, xk[:, 0, chunk(t)], WR[:, k, :, :].rearrange("p a e -> p (a e)"),
                                       start=(k == 0), stop=(k == KC - 1))
                        if k == 0:
                            pe.matmul(o[:, 0:EXPERTS], xk[:, 1, chunk(t)], WR[:, k, 0, :],
                                      start=False, stop=False, skip_group_check=True)
                mm.then_inc(logits_done, 1)

            def low_rank(h, w, bank, ready, n):
                for k in range(KC):
                    pe.wait_ge(ready, n + k + 1)
                    mm = product(PB[bank][:], w, G[:, h, XS + k], chunk(k), k == 0, k == KC - 1)
                mm.then_inc(low_done, 1)

            def base(h, banks, ws, p0, frees):
                for k in range(KC):
                    pe.wait_ge(w_ready, p0 + k + 1)
                    for o in range(KC):
                        if k == 0 and frees[o] is not None:
                            pe.wait_ge(*frees[o])
                        product(PB[banks[o]][:], ws[k], G[:, h, XS + k], chunk(o), k == 0, False)

            def add_low(h, banks, w, low, n):
                pe.wait_ge(low_ready, n)
                for o in range(KC):
                    product(PB[banks[o]][:], w, low, chunk(o), False, True).then_inc(base_done, 1)

            def transpose_gates(h):
                pe.wait_ge(gates_done, h + 1)
                for t in range(TILES):
                    mm = pe.transpose(PB[GATEST[h]][:, chunk(t)], T[:, 0, chunk(t)], sm[:, S_ID:S_ID + P])
                mm.then_inc(gates_t_done, 1)

            pe.wait_ge(warm_ready, 1)
            for _ in range(WARM):
                pe.matmul(PB[LOGITS[1]][:], warm[:, 0:P], warm[:], start=True, stop=True)

            def x_and_w():
                for k in range(KC):
                    pe.wait_ge(x_ready, k + 1)
                    pe.wait_ge(w_ready, P_CW + k + 1)
                    for o in range(KC):
                        product(PB[BASE1[0][o]][:], CW[k], G[:, 0, XS + k], chunk(o), k == 0, False)

            x_and_w()
            logits(0)
            pe.wait_ge(w_ready, P_CA + 1)
            low_rank(0, CA, LOWB[0], x_ready, 0)
            logits(1)
            pe.wait_ge(logits_read, 1)
            transpose_gates(0)
            low_rank(1, CA, LOWB[1], x_ready, KC)
            pe.wait_ge(w_ready, P_CB + 1)
            add_low(0, BASE1[0], CB, GATED[0], 1)
            base(1, BASE1[1], CW, P_CW, [(gates_copied, 1), (low_mul, 1), (logits_read, 2), (base_ready, 1)])
            pe.wait_ge(base_ready, 2)
            transpose_gates(1)

            frees = {0: (base_ready, 3), 1: (base_ready, 4), 2: (low_mul, 2), 3: (gates_copied, 2)}
            for h in range(HALVES):
                for k in range(2):
                    pe.wait_ge(w_ready, (P_UP, P_GATE)[k] + 1)
                    pe.wait_ge(*frees[2 * h + k])
                    for c in range(KC):
                        pe.wait_ge(base_ready, KC * h + c + 1)
                        mm = product(PB[(UPB, GATEB)[k][h]][:], (UPW, GATEW)[k], H[:, h, c], chunk(c), c == 0, c == KC - 1)
                    mm.then_inc(upgate_done, 1)
                if h == 0:
                    add_low(1, BASE1[1], CB, GATED[1], 2)

            def ready_count(h, m):
                return 2 * h + m + 1 if m < 2 else 2 * m + h + 1

            for m, h in [(0, 0), (1, 0), (0, 1), (1, 1)] + [(m, h) for m in range(2, ORDERS + 1) for h in range(HALVES)]:
                pe.wait_ge(w_ready, P_AP + m + 1)
                pe.wait_ge(term_ready, ready_count(h, m))
                for o in range(KC):
                    if m == 0 and h == 0:
                        pe.wait_ge(base_ready, KC + o + 1)
                    if m == 0 and h == 1 and o == 0:
                        pe.wait_ge(delta_done, 3)
                        pe.wait_ge(term_mul, 2)
                    mm = product(PB[APB[h][o]][:], APW[m], G[:, h, m], chunk(o), m == 0, m == ORDERS)
                    if m == ORDERS:
                        mm.then_inc(approx_done, 1)
                if m < 4 and h == 1:
                    mm.then_inc(order_done, 1)

            def ffn_unit(c, par, h, done, g_mul, first):
                for k in range(2):
                    if not first:
                        if k == 0:
                            pe.wait_ge(g_mul, 2 * c + h - 1)
                    for d in range(KC):
                        mm = product(PB[PAIR[h][k]][:], WU[:, 2 * par + k], H[:, h, d], chunk(d), d == 0, d == KC - 1)
                    mm.then_inc(done, 1)

            def ffn1_body(c, par, first=False):
                pe.wait_ge(w_ready, 2 * c + (P_F1 + 2))
                for h in range(HALVES):
                    if first:
                        pe.wait_ge(res_added, KC * 0 + 2 * h + 2)
                    ffn_unit(c, par, h, f1_done, g_mul1, first)

            ffn1_body(0, 0, True)
            ffn1_body(1, 1)
            with pe.Fori(0, (C1 - 2) // 2) as i:
                for par in range(2):
                    ffn1_body(2 * i + (2 + par), par)

            def down(h, j, last, slots, p0, done, g_ready, banks):
                pe.wait_ge(w_ready, p0 + j + 1)
                pe.wait_ge(g_ready, 2 * j + h + 1)
                for o in range(KC):
                    mm = product(PB[banks[o]][:], slots[j], G[:, h, j], chunk(o), j == 0, j == last)
                    if j == last:
                        mm.then_inc(done, 1)

            pe.wait_ge(res_added, HALVES * KC)
            for j in range(C1):
                down(0, j, C1 - 1, DOWN1, P_D1, down1_done, g_ready1, DOWNB[0])
            pe.wait_ge(g_mul1, 2 * C1)
            for j in range(C1):
                down(1, j, C1 - 1, DOWN1, P_D1, down1_done, g_ready1, DOWNB[1])

            pe.wait_ge(lora_ready, 1)
            pe.wait_ge(x1_done, 1)
            low_rank(0, A2S, LOW2B[0], x1_ready, 0)
            base(0, BASE2[0], W2, P_W2, [(x1_done, 2), (x1_done, 3), (x1_done, 4), (x1_done, KC + 1)])
            pe.wait_ge(lora_ready, 2)
            add_low(0, BASE2[0], B2S, MASKED[0], HALVES + 1)
            pe.wait_ge(x1_done, KC + 2)
            low_rank(1, A2S, LOW2B[1], x1_ready, KC)

            def merge_pair(su_n, merged_n):
                pe.wait_ge(su_ready, su_n)
                pe.wait_ge(merged, merged_n)
                for k in range(2):
                    for d in range(KC):
                        mm = pe.matmul(MERGE2[k][:, d, :], S13[:, k, chunk(d)], SU[:, k, :], start=True, stop=True)
                    mm.then_inc(merge_done, 1)

            def merge_down(j, bank):
                pe.matmul(PB[bank][:], S2[:, chunk(j)], S2[:, C2 * P:], start=True, stop=True).then_inc(merge_done, 1)

            pe.wait_ge(stk_ready, 1)
            pe.wait_ge(su_ready, 1)
            for k in range(2):
                pe.wait_ge(base_ready, HALVES * KC + k + 2)
                for d in range(KC):
                    mm = pe.matmul(PB[MERGE[k]][:, chunk(d)], S13[:, k, chunk(d)], SU[:, k, P:], start=True, stop=True)
                mm.then_inc(merge_done, 1)
            base(1, BASE2[1], W2, P_W2, [(x1_done, KC + 3), (x1_done, KC + 4), (low_mul, HALVES + 1), (base_ready, 2 * KC + 1)])
            add_low(1, BASE2[1], B2S, MASKED[1], HALVES + 2)

            for c in range(KC):
                pe.wait_ge(base_ready, HALVES * KC + c + 1)
            pe.wait_ge(low_mul, HALVES + 2)
            pe.wait_ge(w_ready, P_F2 + 2)
            ffn_unit(0, 0, 0, f2_done, g_mul2, True)
            for k in range(2):
                for d in range(KC):
                    pe.wait_ge(base_ready, (HALVES + 1) * KC + d + 1)
                    mm = product(PB[PAIR[1][k]], WU[:, k], H[:, 1, d], chunk(d), d == 0, d == KC - 1)
                mm.then_inc(f2_done, 1)
                if k == 0:
                    merge_pair(2, 2)
            with pe.Fori(0, (C2 - 3) // 2) as i:
                c = 2 * i + 1
                for u in range(2):
                    pe.wait_ge(w_ready, 4 * i + (P_F2 + 2 * (u + 2)))
                    ffn_unit(c + u, (1 + u) % 2, 0, f2_done, g_mul2, False)
                    if u == 0:
                        merge_pair(i + 3, 4 * i + 6)
                    ffn_unit(c + u, (1 + u) % 2, 1, f2_done, g_mul2, False)
            pe.wait_ge(stk_ready, 3)
            for c in range(C2 - 2, C2):
                pe.wait_ge(w_ready, P_F2 + 2 * (c + 1))
                ffn_unit(c, c % 2, 0, f2_done, g_mul2, False)
                for k in range(2):
                    pe.wait_ge(merged, 2 * C2 if c == C2 - 2 else 2 * C2 + k + 1)
                    merge_down(2 * (c - C2 + 2) + k, MERGE[k])
                ffn_unit(c, c % 2, 1, f2_done, g_mul2, False)

            def merge_next(j):
                if j < 6:
                    pe.wait_ge(g_mul2, 2 * C2 - 1)
                else:
                    pe.wait_ge(merged, 2 * C2 + j - 1)
                merge_down(j, j % 2)

            merge_next(4)
            merge_next(5)
            pe.wait_ge(merged, 2 * C2 + 4)
            for j in range(C2):
                if 6 <= j + 4 < C2:
                    merge_next(j + 4)
                down(0, j, C2 - 1, DOWN2, P_D2, down2_done, g_ready2, DOWNB[0])
            pe.wait_ge(g_mul2, 2 * C2)
            for j in range(C2):
                down(1, j, C2 - 1, DOWN2, P_D2, down2_done, g_ready2, DOWNB[1])


def kernel(**inputs):
    import numpy as np
    import concourse.bacc as bacc
    from concourse.bass_utils import run_bass_kernel_spmd

    a = {k: np.asarray(v) for k, v in inputs.items()}

    def by_chunk(w):
        return w.T.reshape(-1, P, w.shape[0]).transpose(1, 0, 2)

    def padded(w, rows):
        return np.concatenate([w, np.zeros((rows - w.shape[0],) + w.shape[1:], w.dtype)])

    xs = a["x"].reshape(HALVES, N, KC, P).transpose(0, 2, 3, 1)
    pieces = list(by_chunk(a["L0_cond_W"]).transpose(1, 0, 2))
    pieces.append(by_chunk(a["L0_cond_A"].reshape(EXPERTS * RANK, D)).reshape(P, D))
    pieces.append(a["L0_cond_B"].transpose(0, 2, 1).reshape(EXPERTS * RANK, D))
    pieces.append(by_chunk(a["L0_attn_up_w"]).reshape(P, D))
    pieces.append(by_chunk(a["L0_attn_gate_w"]).reshape(P, D))
    pieces.append(a["L0_attn_local_approx_output"].T)
    pieces += list(a["L0_attn_fuse_weight"].transpose(2, 1, 0))

    def ffn(gate, up, down, chunks):
        g, u = (by_chunk(padded(w, chunks * P)).reshape(P, KC, chunks, P) for w in (gate, up))
        got = []
        for c in range(chunks):
            got += [g[:, :, c].reshape(P, D), u[:, :, c].reshape(P, D)]
        return got, list(padded(down.T, chunks * P).reshape(chunks, P, D))

    ups1, downs1 = ffn(a["L0_attn_ffn_gate_w"], a["L0_attn_ffn_up_w"], a["L0_attn_ffn_down_w"], C1)
    ups2, downs2 = ffn(a["L0_ffn_w1"], a["L0_ffn_w3"], a["L0_ffn_w2"], C2)
    pieces += ups1 + downs1 + list(by_chunk(a["L0_cond2_W"]).transpose(1, 0, 2)) + ups2 + downs2
    pieces = np.stack(pieces)

    def stacked(w):
        return np.concatenate([padded(w, 32)] * 3)

    b1, b3 = (np.concatenate([np.zeros((KS, P), np.float32), stacked(padded(a[k], C2 * P).T)], axis=1)
              .reshape(KS, (C2 + 1) // 2, 2 * P) for k in ("L0_ffn_lora_B1", "L0_ffn_lora_B3"))
    small = np.concatenate([
        by_chunk(a["L0_cond_Wr"]).reshape(P, KC * EXPERTS),
        a["L0_attn_local_point"].reshape(P, 1),
        a["L0_cond2_b"].reshape(KC, P).T,
        np.broadcast_to(a["L0_attn_discount_factor"], (P, ORDERS)),
        np.broadcast_to((EXPERTS - np.arange(EXPERTS)).astype(np.float32), (P, EXPERTS)),
        np.broadcast_to(np.arange(EXPERTS).astype(np.float32), (P, EXPERTS)),
        np.equal.outer(np.arange(P) // RANK, np.arange(BATCH)).astype(np.float32),
        np.eye(P, dtype=np.float32),
    ], axis=1)
    arrays = {
        "x": xs,
        "ids_b": np.broadcast_to(a["itok_B_0_7"], (P, BATCH)),
        "slot_ids": a["itok_B_0_23"].reshape(1, BATCH),
        "small": small,
        "pieces": pieces,
        "lora_a": a["L0_cond2_lora_As"].reshape(SLOTS, KC, P, RANK).transpose(0, 2, 1, 3).reshape(SLOTS, P, KC * RANK),
        "lora_b": a["L0_cond2_lora_Bs"],
        "stk13": np.stack([stacked(a["L0_ffn_lora_A1"]), stacked(a["L0_ffn_lora_A3"])], axis=1),
        "stk2": np.concatenate([stacked(padded(a["L0_ffn_lora_A2"].T, C2 * P).T), stacked(a["L0_ffn_lora_B2"].T)], axis=1),
        "stk_up": np.stack([b1, b3], axis=2).transpose(1, 0, 2, 3),
    }
    nc = bacc.Bacc("TRN2", target_bir_lowering=False, num_devices=1)
    given, args = {}, []
    for name, v in arrays.items():
        v = np.ascontiguousarray(v)
        given[f"in_{name}"] = v
        args.append(nc.dram_tensor(f"in_{name}", v.shape, mybir.dt.from_np(v.dtype), kind="ExternalInput").ap())
    args.append(nc.dram_tensor("out_x", (HALVES, KC, P, N), F32, kind="ExternalOutput").ap())
    build(nc, *args)
    got = run_bass_kernel_spmd(nc, [given], core_ids=[0]).results[0]["out_x"]
    return got.transpose(0, 3, 1, 2).reshape(BATCH, SEQ, D)
```

```python
from contextlib import ExitStack

import concourse.bass as bass
from concourse import mybir

ALU = mybir.AluOpType
ACT = mybir.ActivationFunctionType
AX = mybir.AxisListType
F32 = mybir.dt.float32
F32R = mybir.dt.float32r
I32 = mybir.dt.int32
BF16 = mybir.dt.bfloat16

P = 128
BATCH, SEQ, D = 8, 128, 512
TOKENS = BATCH * SEQ
HALVES = 2
N = TOKENS // HALVES
TILES = N // P
KC = D // P
EXPERTS, RANK = 8, 16
SLOTS = 32
ORDERS = 6
THD = 2.5
F1, F2 = 1248, 1376
C1, C2 = -(-F1 // P), -(-F2 // P)
SCALING = 2.0
LANG_BIAS = 5.0
BIG = 3.0e38

P_CW = 0
P_CA = P_CW + KC
P_CB = P_CA + 1
P_UP = P_CB + 1
P_GATE = P_UP + 1
P_AP = P_GATE + 1
P_F1 = P_AP + 1 + ORDERS
P_D1 = P_F1 + 2 * C1
P_W2 = P_D1 + C1
P_F2 = P_W2 + KC
P_D2 = P_F2 + 2 * C2
PIECES = P_D2 + C2
WARM = 11
RING = 4

KS = 96
LO_A = slice(64, 96)
LO_B = slice(32, 64)

S_WR = 0
S_LP = S_WR + KC * EXPERTS
S_B2 = S_LP + 1
S_DISC = S_B2 + KC
S_REV = S_DISC + ORDERS
S_IOTA = S_REV + EXPERTS
S_MASK = S_IOTA + EXPERTS
S_ID = S_MASK + BATCH
S_COLS = S_ID + P


FIRST = ([("x", 0, 0), ("w", 0, 0)] + [("x", 0, c) for c in range(1, KC)]
         + [("w", 0, 1), ("x", 1, 0), ("x", 1, 1), ("w", 0, 2), ("x", 1, 2), ("x", 1, 3), ("w", 0, 3)])


def x_count(h, c):
    return [(g, k) for kind, g, k in FIRST if kind == "x"].index((h, c)) + 1


def build(nc, x, ids_b, slot_ids, small, pieces, lora_a, lora_b, stk13, stk2, stk_up, out):
    with ExitStack() as ctx:
        def sb(name, shape, dt=F32):
            return ctx.enter_context(nc.sbuf_tensor(name, shape, dt))

        def sem(name):
            return ctx.enter_context(nc.semaphore(name))

        X = sb("X", [P, HALVES, KC, N])
        H = sb("H", [P, HALVES, KC, 2, N], F32R)
        G = sb("G", [P, HALVES, 11, 2, N], F32R)
        WU = sb("WU", [P, 4, 2, N], F32R)
        raw = sb("raw", [P, RING, N])
        T = sb("T", [P, 8, N])
        ga_raw = sb("ga_raw", [P, BATCH * KC * RANK])
        gb_raw = sb("gb_raw", [P, D])
        sm = sb("sm", [P, S_COLS])
        idb = sb("idb", [P, BATCH], I32)
        idf = sb("idf", [P, BATCH])
        slot_i = sb("slot_i", [1, BATCH], I32)
        slot_f = sb("slot_f", [1, 3, BATCH])
        slot_ok = sb("slot_ok", [1, BATCH], I32)
        LT = sb("LT", [2 * EXPERTS, HALVES, N])
        WR = sb("WR", [P, KC, 2, EXPERTS], F32R)
        warm = sb("warm", [P, N], BF16)
        unused = sb("unused", [P, 1])
        coef = sb("coef", [P, ORDERS])
        lang = sb("lang", [P, BATCH, EXPERTS])
        S13 = sb("S13", [KS, 2, D], F32R)
        S2 = sb("S2", [KS, C2 * P + D], F32R)
        SU = sb("SU", [KS, 2, 2 * P], F32R)
        su_raw = sb("su_raw", [KS, 2, 2 * P])
        lg = sb("lg", [P, BATCH, EXPERTS])
        lg2 = sb("lg2", [P, BATCH, EXPERTS])
        eq = sb("eq", [P, 2, BATCH, EXPERTS])
        one1 = sb("one1", [P, BATCH, EXPERTS])
        one2 = sb("one2", [P, BATCH, EXPERTS])
        col = sb("col", [P, 8, BATCH])

        PS = ctx.enter_context(nc.psum_tensor("PS", [P, 8, N], F32))
        PB = [PS[:, i, :] for i in range(8)]

        XS = 7
        CW = [G[:, 1, k] for k in range(KC)]
        CA, CB, UPW, GATEW = G[:, 1, 4], G[:, 0, 3], G[:, 1, 5], G[:, 1, 6]
        GATED = [G[:, 0, 4], G[:, 0, 5]]
        APW = [WU[:, m] for m in range(4)] + [G[:, 0, XS + m] for m in range(3)]
        W2 = [G[:, 0, k] for k in range(KC)]
        A2S, B2S = G[:, 0, 4], G[:, 0, 5]
        MASKED = [G[:, 1, 0], G[:, 1, 1]]
        DOWN1 = [WU[:, j] for j in range(4)] + [H[:, j // KC, j % KC] for j in range(C1 - 4)]
        DOWN2 = [WU[:, (j + 2) % 4] for j in range(4)] + [H[:, j // KC, j % KC] for j in range(C2 - 4)]

        LOGITS, LOWB, GATEST = (0, 2), (1, 6), (2, 0)
        LOGITST = LOGITS[0]
        BASE1 = ((3, 7, 4, 5), (0, 1, 2, 3))
        UPB, GATEB = (4, 6), (5, 7)
        APB = ((0, 1, 2, 3), (4, 5, 6, 7))
        PAIR = ((0, 1), (2, 3))
        DOWNB = ((4, 5, 6, 7), (0, 1, 2, 3))
        LOW2B = (4, 1)
        BASE2 = ((5, 6, 7, 0), (2, 3, 4, 5))
        MERGE = (6, 7)
        MERGE2 = [PS[:, 4 + 2 * k:6 + 2 * k, :].rearrange("p b (a n) -> p (b a) n", a=2) for k in range(2)]

        x_in = [[sem(f"x_in{h}{c}") for c in range(KC)] for h in range(HALVES)]
        small_in = sem("small_in")
        ids_in = sem("ids_in")
        slots_in = sem("slots_in")
        raw_in = [sem(f"raw_in{s}") for s in range(RING)]
        lora_a_in, lora_b_in = sem("lora_a_in"), sem("lora_b_in")
        stk_in = sem("stk_in")
        su_in = sem("su_in")
        out_done = sem("out_done")
        warm_ready = sem("warm_ready")
        logits_t_done = sem("logits_t_done")
        logits_done = sem("logits_done")
        low_done = sem("low_done")
        gates_t_done = sem("gates_t_done")
        base_done = sem("base_done")
        upgate_done = sem("upgate_done")
        order_done = sem("order_done")
        approx_done = sem("approx_done")
        f1_done, f2_done = sem("f1_done"), sem("f2_done")
        down1_done, down2_done = sem("down1_done"), sem("down2_done")
        merge_done = sem("merge_done")
        hi_w = sem("hi_w")
        hi_x = sem("hi_x")
        hi_wr = sem("hi_wr")
        hi_low = sem("hi_low")
        hi_base = sem("hi_base")
        hi_term = sem("hi_term")
        hi_g1, hi_g2 = sem("hi_g1"), sem("hi_g2")
        silu1, silu2 = sem("silu1"), sem("silu2")
        hi_x1 = sem("hi_x1")
        hi_lora = sem("hi_lora")
        hi_stk = sem("hi_stk")
        hi_su = sem("hi_su")
        coef_done = sem("coef_done")
        logits_copied = sem("logits_copied")
        exp_done = sem("exp_done")
        gates_copied = sem("gates_copied")
        abs_done = sem("abs_done")
        wr_ready = sem("wr_ready")
        lang_done = sem("lang_done")
        slots_ok = sem("slots_ok")
        w_ready = sem("w_ready")
        x_ready = sem("x_ready")
        low_mul = sem("low_mul")
        low_ready = sem("low_ready")
        base_ready = sem("base_ready")
        logits_read = sem("logits_read")
        gap_done = sem("gap_done")
        gates_done = sem("gates_done")
        delta_done = sem("delta_done")
        term_mul = sem("term_mul")
        term_ready = sem("term_ready")
        res_added = sem("res_added")
        g_mul1, g_mul2 = sem("g_mul1"), sem("g_mul2")
        g_ready1, g_ready2 = sem("g_ready1"), sem("g_ready2")
        x1_done = sem("x1_done")
        x1_ready = sem("x1_ready")
        lora_ready = sem("lora_ready")
        stk_ready = sem("stk_ready")
        su_ready = sem("su_ready")
        merged = sem("merged")
        out_ready = sem("out_ready")
        dve_step = sem("dve_step")

        def f32(ap):
            return ap.bitcast(F32)

        def raw_slot(p):
            return raw[:, p % RING, :]

        def raw_count(p):
            return 16 * (p // RING + 1)

        def term_count(h, m):
            return 2 * (m - 1) + h + 1

        block = ctx.enter_context(nc.Block())

        @block.sync
        def _(sp):
            for kind, h, c in FIRST:
                if kind == "x":
                    sp.dma_start(X[:, h, c, :], x[h, c]).then_inc(x_in[h][c], 16)
                else:
                    sp.dma_start(raw_slot(P_CW + c), pieces[P_CW + c]).then_inc(raw_in[P_CW + c], 16)
            whole = (PIECES - RING) // RING
            with sp.Fori(0, whole) as i:
                for s in range(RING):
                    sp.wait_ge(w_ready, i * RING + s + 1)
                    sp.dma_start(raw[:, s, :], pieces[i * RING + RING + s]).then_inc(raw_in[s], 16)
            for p in range(RING * (whole + 1), PIECES):
                sp.wait_ge(w_ready, p - RING + 1)
                sp.dma_start(raw_slot(p), pieces[p]).then_inc(raw_in[p % RING], 16)
            for h in range(HALVES):
                for c in range(KC):
                    sp.wait_ge(out_ready, KC * h + c + 1)
                    sp.dma_start(out[h, c], X[:, h, c, :]).then_inc(out_done, 16)
            sp.wait_ge(out_done, 16 * HALVES * KC)

        @block.gpsimd
        def _(pool):
            pool.memset(warm[:], 0.0).then_inc(warm_ready, 1)
            pool.dma_start(sm[:], small).then_inc(small_in, 16)
            pool.dma_start(idb[:], ids_b).then_inc(ids_in, 16)
            pool.dma_start(slot_i[:], slot_ids).then_inc(slots_in, 16)
            pool.wait_ge(slots_ok, 1)
            for b in range(BATCH):
                s = pool.value_load(slot_ok[0:1, b:b + 1], min_val=0, max_val=SLOTS - 1)
                pool.dma_start(ga_raw[:, b * KC * RANK:(b + 1) * KC * RANK], lora_a[s]).then_inc(lora_a_in, 16)
                pool.dma_start(gb_raw[b * RANK:(b + 1) * RANK, :], lora_b[s]).then_inc(lora_b_in, 16)
            pool.dma_start(su_raw[:], stk_up[0]).then_inc(su_in, 16)
            pool.wait_ge(term_ready, 2 * (ORDERS + 1))
            pool.dma_start(T[0:KS, 4:6, :], stk13).then_inc(stk_in, 16)
            pool.wait_ge(stk_ready, 1)
            pool.dma_start(T[0:KS, 4:8, :].rearrange("p a n -> p (a n)")[:, 0:C2 * P + D], stk2).then_inc(stk_in, 16)
            for q in range(1, (C2 + 1) // 2):
                pool.wait_ge(su_ready, q)
                pool.dma_start(su_raw[:], stk_up[q]).then_inc(su_in, 16)

        @block.scalar
        def _(act):

            def copy(o, i):
                return nc.scalar.activation(o, i, ACT.Copy)

            def x_hi(h, c):
                act.wait_ge(x_in[h][c], 16)
                copy(G[:, h, XS + c, 0, :], X[:, h, c, :]).then_inc(hi_x, 1)

            def w_hi(p, dst):
                act.wait_ge(raw_in[p % RING], raw_count(p))
                copy(dst[:, 0, :], raw_slot(p)).then_inc(hi_w, 1)

            def gate_low(h):
                act.wait_ge(low_mul, h + 1)
                copy(GATED[h][:, 0, :], T[:, 2 + h, :]).then_inc(hi_low, 1)

            def base_hi(h, c):
                act.wait_ge(base_done, KC * h + c + 1)
                copy(H[:, h, c, 0, :], PB[BASE1[h][c]][:]).then_inc(hi_base, 1)

            act.wait_ge(warm_ready, 1)
            nc.scalar.activation(unused[:], warm[:, 0:1], ACT.Exp)

            for kind, h, c in FIRST:
                if kind == "x":
                    x_hi(h, c)
                else:
                    w_hi(P_CW + c, CW[c])
                if (kind, c) == ("w", 0):
                    act.wait_ge(small_in, 16)
                    copy(WR[:, :, 0, :], sm[:, S_WR:S_WR + KC * EXPERTS].rearrange("p (k e) -> p k e", k=KC)).then_inc(hi_wr, 1)
            w_hi(P_CA, CA)
            w_hi(P_CB, CB)
            nc.scalar.activation(coef[:], sm[:, S_DISC:S_DISC + ORDERS], ACT.Exp, scale=-1.0).then_inc(coef_done, 1)
            for h in range(HALVES):
                act.wait_ge(logits_t_done, h + 1)
                copy(LT[:, h, :], PB[LOGITS[h]][0:2 * EXPERTS, :]).then_inc(logits_copied, 1)
            act.wait_ge(gap_done, 1)
            nc.scalar.activation(col[:, 5, :], col[:, 4, :], ACT.Exp).then_inc(exp_done, 1)
            for h in range(HALVES):
                act.wait_ge(gates_t_done, h + 1)
                copy(T[:, h, :], PB[GATEST[h]][:]).then_inc(gates_copied, 1)
            for h in range(HALVES):
                gate_low(h)
            for c in range(KC):
                base_hi(0, c)
            w_hi(P_UP, UPW)
            w_hi(P_GATE, GATEW)
            act.wait_ge(coef_done, 1)
            for m in range(ORDERS + 1):
                p = P_AP + m
                act.wait_ge(raw_in[p % RING], raw_count(p))
                if m >= 4:
                    act.wait_ge(base_done, KC)
                scale = coef[:, m - 1:m] if m else 1.0
                nc.scalar.activation(APW[m][:, 0, :], raw_slot(p), ACT.Copy, scale=scale).then_inc(hi_w, 1)

            def term_hi(h, m):
                if m == 0:
                    act.wait_ge(upgate_done, 2 * h + 1)
                    src = PB[UPB[h]][:]
                else:
                    act.wait_ge(term_mul, term_count(h, m))
                    src = T[:, 4 + 2 * h + m % 2, :]
                copy(G[:, h, m, 0, :], src).then_inc(hi_term, 1)

            for h in range(HALVES):
                term_hi(h, 0)
                if h == 0:
                    for c in range(KC):
                        base_hi(1, c)
                act.wait_ge(delta_done, 2 * h + 1)
                nc.scalar.activation(T[:, 2 + h, :], T[:, h, :], ACT.Abs).then_inc(abs_done, 1)
                term_hi(h, 1)
            for m in range(2, ORDERS + 1):
                for h in range(HALVES):
                    term_hi(h, m)

            def ffn_unit(c, h, done, silu, g_mul, hi_g, first):
                act.wait_ge(done, 4 * c + 2 * h + 1)
                if not first:
                    act.wait_ge(g_mul, 2 * c + h - 1)
                nc.scalar.activation(T[:, h, :], PB[PAIR[h][0]][:], ACT.Silu).then_inc(silu, 1)
                act.wait_ge(g_mul, 2 * c + h + 1)
                copy(G[:, h, c, 0, :] if isinstance(c, int) else G[:, h, bass.ds(c, 1), 0, :],
                     T[:, 2 + h, :]).then_inc(hi_g, 1)

            for c in range(2):
                for k in range(2):
                    act.wait_ge(order_done, 2 * c + k + 1)
                    w_hi(P_F1 + 2 * c + k, WU[:, 2 * c + k])

            def ffn1_body(c, par, count):
                for h in range(HALVES):
                    ffn_unit(c, h, f1_done, silu1, g_mul1, hi_g1, False if not isinstance(c, int) else c == 0)
                act.wait_ge(f1_done, 4 * c + 4)
                for k in range(2):
                    s, n = count(k)
                    act.wait_ge(raw_in[s], n)
                    copy(WU[:, 2 * par + k, 0, :], raw[:, s, :]).then_inc(hi_w, 1)

            def static_count(p0):
                return lambda k: ((p0 + k) % RING, raw_count(p0 + k))

            for c in range(2):
                ffn1_body(c, c, static_count(P_F1 + 2 * (c + 2)))
            with act.Fori(0, (C1 - 2) // 2) as i:
                for par in range(2):
                    p0 = P_F1 + 2 * (2 + par + 2)
                    ffn1_body(2 * i + (2 + par), par,
                              lambda k, p0=p0: ((p0 + k) % RING, i * 16 + raw_count(p0 + k)))
            for j in range(4, C1):
                w_hi(P_D1 + j, DOWN1[j])

            act.wait_ge(stk_in, 16)
            copy(S13[:], T[0:KS, 4:6, :]).then_inc(hi_stk, 1)
            act.wait_ge(stk_in, 32)
            stk_flat = T[0:KS, 4:8, :].rearrange("p a n -> p (a n)")[:, 0:C2 * P + D]
            copy(S2[:], stk_flat).then_inc(hi_stk, 1)

            def x1_hi(h):
                act.wait_ge(down1_done, KC * (h + 1))
                for c in range(KC):
                    act.wait_ge(x1_done, KC * h + c + 1)
                    copy(G[:, h, XS + c, 0, :], X[:, h, c, :]).then_inc(hi_x1, 1)

            x1_hi(0)
            act.wait_ge(lora_a_in, 16 * BATCH)
            copy(A2S[:, 0, :].rearrange("p (k b r) -> p k b r", k=KC, b=BATCH),
                 ga_raw[:].rearrange("p (b k r) -> p k b r", k=KC, b=BATCH)).then_inc(hi_lora, 1)
            for k in range(KC):
                w_hi(P_W2 + k, W2[k])
            act.wait_ge(lora_b_in, 16 * BATCH)
            copy(B2S[:, 0, :], gb_raw[:]).then_inc(hi_lora, 1)
            x1_hi(1)

            def su_hi(landed):
                act.wait_ge(su_in, landed)
                copy(SU[:], su_raw[:]).then_inc(hi_su, 1)

            su_hi(16)

            def low_hi(h):
                act.wait_ge(low_mul, HALVES + h + 1)
                copy(MASKED[h][:, 0, :], T[:, h, :]).then_inc(hi_low, 1)

            def base2_hi(h, c):
                act.wait_ge(base_done, KC * (HALVES + h) + c + 1)
                nc.scalar.activation(H[:, h, c, 0, :], PB[BASE2[h][c]][:], ACT.Identity,
                                     bias=sm[:, S_B2 + c:S_B2 + c + 1]).then_inc(hi_base, 1)

            def merged_hi(c, par, slot):
                for k in range(2):
                    act.wait_ge(merged, 2 * c + k + 1)
                    copy(WU[:, 2 * par + k, 0, :], raw[:, slot(k), :]).then_inc(hi_w, 1)

            def slot_of(c):
                return lambda k: (P_F2 + 2 * c + k) % RING

            low_hi(0)
            for c in range(KC):
                base2_hi(0, c)
            low_hi(1)
            merged_hi(0, 0, slot_of(0))
            act.wait_ge(merge_done, 2)
            su_hi(32)
            for c in range(KC):
                base2_hi(1, c)

            def unit2(c, h, first=False):
                ffn_unit(c, h, f2_done, silu2, g_mul2, hi_g2, first)

            unit2(0, 0, True)
            merged_hi(1, 1, slot_of(1))
            unit2(0, 1, True)
            act.wait_ge(f2_done, 4)
            merged_hi(2, 0, slot_of(2))
            with act.Fori(0, (C2 - 3) // 2) as i:
                c = 2 * i + 1
                act.wait_ge(merge_done, 2 * i + 4)
                su_hi(i * 16 + 48)
                for u in range(2):
                    for h in range(HALVES):
                        unit2(c + u, h)
                    act.wait_ge(f2_done, 4 * c + (4 * u + 4))
                    merged_hi(c + (u + 2), (1 + u) % 2, slot_of(3 + u))
            for c in range(C2 - 2, C2):
                for h in range(HALVES):
                    unit2(c, h)
                act.wait_ge(f2_done, 4 * c + 4)
                merged_hi(c + 2, c % 2, slot_of(c + 2))
            for j in range(4, C2):
                act.wait_ge(merged, 2 * C2 + j + 1)
                copy(DOWN2[j][:, 0, :], raw_slot(P_D2 + j)).then_inc(hi_w, 1)

        @block.vector
        def _(dve):
            steps = [0]

            def step(ins):
                steps[0] += 1
                ins.then_inc(dve_step, 1)
                dve.wait_ge(dve_step, steps[0])

            V = nc.vector

            def lo(dst, full, hi):
                return V.tensor_tensor(dst, full, f32(hi), ALU.subtract)

            def x_lo(h, c):
                dve.wait_ge(hi_x, KC * h + c + 1)
                lo(G[:, h, XS + c, 1, :], X[:, h, c, :], G[:, h, XS + c, 0, :]).then_inc(x_ready, 1)

            def w_lo(p, dst):
                dve.wait_ge(hi_w, p + 1)
                lo(dst[:, 1, :], raw_slot(p), dst[:, 0, :]).then_inc(w_ready, 1)

            def small_col(a, n=1):
                return sm[:, a:a + n]

            full = [P, BATCH, EXPERTS]

            def over_e(ap):
                return ap.unsqueeze(2).to_broadcast(full)

            rev = small_col(S_REV, EXPERTS).unsqueeze(1).to_broadcast(full)

            def first_max(logits, m, k, one):
                step(V.tensor_reduce(col[:, m, :], logits, AX.X, ALU.max))
                step(V.tensor_tensor(eq[:, 0], logits, over_e(col[:, m, :]), ALU.is_equal))
                step(V.tensor_tensor(eq[:, 1], eq[:, 0], rev, ALU.mult))
                step(V.tensor_reduce(col[:, k, :], eq[:, 1], AX.X, ALU.max))
                step(V.tensor_tensor(one, rev, over_e(col[:, k, :]), ALU.is_equal))

            def route():
                dve.wait_ge(logits_done, 1)
                ps = PB[LOGITST][:, 0:BATCH * 2 * EXPERTS].rearrange("p (t a e) -> p t a e", t=BATCH, a=2)
                step(V.scalar_tensor_tensor(lg2[:], lang[:], LANG_BIAS, ps[:, :, 0, :], ALU.mult, ALU.add))
                V.tensor_tensor(lg[:], ps[:, :, 1, :], lg2[:], ALU.add).then_inc(logits_read, 1)
                dve.wait_ge(logits_read, 1)
                first_max(lg[:], 0, 1, one1[:])
                step(V.scalar_tensor_tensor(lg2[:], one1[:], -BIG, lg[:], ALU.mult, ALU.add))
                first_max(lg2[:], 2, 3, one2[:])
                V.tensor_tensor(col[:, 4, :], col[:, 2, :], col[:, 0, :], ALU.subtract).then_inc(gap_done, 1)

            def gates():
                dve.wait_ge(exp_done, 1)
                step(V.tensor_scalar(col[:, 6, :], col[:, 5, :], 1.0, 1.0 / SCALING, ALU.add, ALU.mult))
                step(V.reciprocal(col[:, 6, :], col[:, 6, :]))
                step(V.tensor_tensor(col[:, 7, :], col[:, 5, :], col[:, 6, :], ALU.mult))
                step(V.tensor_tensor(one1[:], one1[:], over_e(col[:, 6, :]), ALU.mult))
                step(V.tensor_tensor(one2[:], one2[:], over_e(col[:, 7, :]), ALU.mult))
                step(V.tensor_tensor(one1[:], one1[:], one2[:], ALU.add))
                for h in range(HALVES):
                    own = one1[:, TILES * h:TILES * (h + 1), :].rearrange("p t e -> p (t e)").unsqueeze(2)
                    V.tensor_copy(T[:, 4 + h, :].rearrange("p (a r) -> p a r", r=RANK),
                                  own.to_broadcast([P, TILES * EXPERTS, RANK])).then_inc(gates_done, 1)

            def gate_low(h):
                dve.wait_ge(low_done, h + 1)
                dve.wait_ge(gates_copied, h + 1)
                V.tensor_tensor(T[:, 2 + h, :], PB[LOWB[h]][:], T[:, h, :], ALU.mult).then_inc(low_mul, 1)
                dve.wait_ge(hi_low, h + 1)
                lo(GATED[h][:, 1, :], T[:, 2 + h, :], GATED[h][:, 0, :]).then_inc(low_ready, 1)

            def base_lo(h, c):
                dve.wait_ge(hi_base, KC * h + c + 1)
                lo(H[:, h, c, 1, :], PB[BASE1[h][c]][:], H[:, h, c, 0, :]).then_inc(base_ready, 1)

            for kind, h, c in FIRST:
                if kind == "x":
                    x_lo(h, c)
                else:
                    w_lo(P_CW + c, CW[c])
                if (kind, c) == ("w", 0):
                    dve.wait_ge(hi_wr, 1)
                    lo(WR[:, :, 1, :], sm[:, S_WR:S_WR + KC * EXPERTS].rearrange("p (k e) -> p k e", k=KC),
                       WR[:, :, 0, :]).then_inc(wr_ready, 1)
            dve.wait_ge(ids_in, 16)
            step(V.tensor_copy(idf[:], idb[:]))
            V.tensor_tensor(lang[:], sm[:, S_IOTA:S_IOTA + EXPERTS].unsqueeze(1).to_broadcast([P, BATCH, EXPERTS]),
                            idf[:].unsqueeze(2).to_broadcast([P, BATCH, EXPERTS]), ALU.is_equal).then_inc(lang_done, 1)
            dve.wait_ge(lang_done, 1)
            w_lo(P_CA, CA)
            w_lo(P_CB, CB)
            route()
            gates()
            gate_low(0)
            gate_low(1)
            for c in range(KC):
                base_lo(0, c)
            dve.wait_ge(slots_in, 16)
            step(V.tensor_copy(slot_f[:, 0, :], slot_i[:]))
            step(V.tensor_scalar(slot_f[:, 1, :], slot_f[:, 0, :], 0.0, float(SLOTS), ALU.is_lt, ALU.mult))
            step(V.tensor_tensor(slot_f[:, 2, :], slot_f[:, 0, :], slot_f[:, 1, :], ALU.add))
            V.tensor_scalar(slot_ok[:], slot_f[:, 2, :], 0.0, SLOTS - 1.0, ALU.max, ALU.min).then_inc(slots_ok, 1)
            w_lo(P_UP, UPW)
            w_lo(P_GATE, GATEW)
            dve.wait_ge(coef_done, 1)
            for m in range(ORDERS + 1):
                p = P_AP + m
                dve.wait_ge(hi_w, p + 1)
                if m == 0:
                    lo(APW[m][:, 1, :], raw_slot(p), APW[m][:, 0, :]).then_inc(w_ready, 1)
                else:
                    V.scalar_tensor_tensor(APW[m][:, 1, :], raw_slot(p), coef[:, m - 1:m], f32(APW[m][:, 0, :]),
                                           ALU.mult, ALU.subtract).then_inc(w_ready, 1)

            def term(h, m):
                q = T[:, 4 + 2 * h + m % 2, :]
                if m == 1:
                    a, b = PB[UPB[h]][:], T[:, h, :]
                else:
                    a, b = T[:, 4 + 2 * h + (m - 1) % 2, :], T[:, 2 + h if m == 5 else h, :]
                    dve.wait_ge(term_mul, term_count(h, m - 1))
                V.tensor_tensor(q, a, b, ALU.mult).then_inc(term_mul, 1)

            lows = [0]

            def term_lo(h, m):
                lows[0] += 1
                dve.wait_ge(hi_term, lows[0])
                src = T[:, 4 + 2 * h + m % 2, :] if m else PB[UPB[h]][:]
                lo(G[:, h, m, 1, :], src, G[:, h, m, 0, :]).then_inc(term_ready, 1)

            for h in range(HALVES):
                term_lo(h, 0)
                if h == 0:
                    for c in range(KC):
                        base_lo(1, c)
                dve.wait_ge(upgate_done, 2 * h + 2)
                V.tensor_scalar(T[:, h, :], PB[GATEB[h]][:], small_col(S_LP), None, ALU.subtract).then_inc(delta_done, 1)
                dve.wait_ge(delta_done, 2 * h + 1)
                term(h, 1)
                dve.wait_ge(abs_done, h + 1)
                V.scalar_tensor_tensor(T[:, 2 + h, :], T[:, 2 + h, :], THD, T[:, h, :], ALU.is_le,
                                       ALU.mult).then_inc(delta_done, 1)
                term_lo(h, 1)
            for m in range(2, ORDERS + 1):
                for h in range(HALVES):
                    if m == 5:
                        dve.wait_ge(delta_done, 2 * h + 2)
                    term(h, m)
                for h in range(HALVES):
                    term_lo(h, m)

            for c in range(2):
                for k in range(2):
                    w_lo(P_F1 + 2 * c + k, WU[:, 2 * c + k])
            for h in range(HALVES):
                for c in range(KC):
                    dve.wait_ge(approx_done, KC * h + c + 1)
                    V.tensor_tensor(X[:, h, c, :], PB[APB[h][c]][:], X[:, h, c, :], ALU.add).then_inc(res_added, 1)

            def ffn_unit(c, h, done, silu, g_mul, hi_g, g_ready):
                dve.wait_ge(done, 4 * c + 2 * h + 2)
                dve.wait_ge(silu, 2 * c + h + 1)
                V.tensor_tensor(T[:, 2 + h, :], PB[PAIR[h][1]][:], T[:, h, :], ALU.mult).then_inc(g_mul, 1)
                dve.wait_ge(hi_g, 2 * c + h + 1)
                g = G[:, h, c, :, :] if isinstance(c, int) else G[:, h, bass.ds(c, 1), :, :].rearrange("p a b n -> p (a b) n")
                lo(g[:, 1, :], T[:, 2 + h, :], g[:, 0, :]).then_inc(g_ready, 1)

            def split_up(n0, par, slot):
                for k in range(2):
                    dve.wait_ge(hi_w, n0 + k)
                    lo(WU[:, 2 * par + k, 1, :], raw[:, slot(k), :], WU[:, 2 * par + k, 0, :]).then_inc(w_ready, 1)

            def ffn1_body(c, par):
                for h in range(HALVES):
                    ffn_unit(c, h, f1_done, silu1, g_mul1, hi_g1, g_ready1)
                split_up(2 * c + (P_F1 + 4 + 1), par, lambda k: (P_F1 + 2 * (par + 2) + k) % RING)

            for c in range(2):
                ffn1_body(c, c)
            with dve.Fori(0, (C1 - 2) // 2) as i:
                for par in range(2):
                    ffn1_body(2 * i + (2 + par), par)
            for j in range(4, C1):
                w_lo(P_D1 + j, DOWN1[j])

            dve.wait_ge(hi_stk, 1)
            V.tensor_tensor(S13[LO_A], T[LO_A, 4:6, :], f32(S13[LO_A]), ALU.subtract).then_inc(stk_ready, 1)
            dve.wait_ge(hi_stk, 2)
            stk_flat = T[0:KS, 4:8, :].rearrange("p a n -> p (a n)")
            V.tensor_tensor(S2[LO_A, 0:C2 * P], stk_flat[LO_A, 0:C2 * P], f32(S2[LO_A, 0:C2 * P]),
                            ALU.subtract).then_inc(stk_ready, 1)
            V.tensor_tensor(S2[LO_B, C2 * P:], stk_flat[LO_B, C2 * P:C2 * P + D], f32(S2[LO_B, C2 * P:]),
                            ALU.subtract).then_inc(stk_ready, 1)

            def x1(h):
                for c in range(KC):
                    dve.wait_ge(down1_done, KC * h + c + 1)
                    dve.wait_ge(res_added, KC * h + c + 1)
                    V.tensor_tensor(X[:, h, c, :], PB[DOWNB[h][c]][:], X[:, h, c, :], ALU.add).then_inc(x1_done, 1)
                for c in range(KC):
                    dve.wait_ge(hi_x1, KC * h + c + 1)
                    lo(G[:, h, XS + c, 1, :], X[:, h, c, :], G[:, h, XS + c, 0, :]).then_inc(x1_ready, 1)

            x1(0)
            dve.wait_ge(hi_lora, 1)
            lo(A2S[:, 1, :].rearrange("p (k b r) -> p k b r", k=KC, b=BATCH),
               ga_raw[:].rearrange("p (b k r) -> p k b r", k=KC, b=BATCH),
               A2S[:, 0, :].rearrange("p (k b r) -> p k b r", k=KC, b=BATCH)).then_inc(lora_ready, 1)
            for k in range(KC):
                w_lo(P_W2 + k, W2[k])
            dve.wait_ge(hi_lora, 2)
            lo(B2S[:, 1, :], gb_raw[:], B2S[:, 0, :]).then_inc(lora_ready, 1)
            x1(1)

            def su_lo(n):
                dve.wait_ge(hi_su, n)
                V.tensor_tensor(SU[LO_B], su_raw[LO_B], f32(SU[LO_B]), ALU.subtract).then_inc(su_ready, 1)

            su_lo(1)

            def mask_low(h):
                dve.wait_ge(low_done, HALVES + h + 1)
                mask = sm[:, S_MASK + TILES * h:S_MASK + TILES * (h + 1)].unsqueeze(2).to_broadcast([P, TILES, P])
                V.scalar_tensor_tensor(T[:, h, :].rearrange("p (t n) -> p t n", t=TILES),
                                       PB[LOW2B[h]][:].rearrange("p (t n) -> p t n", t=TILES), SCALING, mask,
                                       ALU.mult, ALU.mult).then_inc(low_mul, 1)
                dve.wait_ge(hi_low, HALVES + h + 1)
                lo(MASKED[h][:, 1, :], T[:, h, :], MASKED[h][:, 0, :]).then_inc(low_ready, 1)

            def base2_lo(h, c):
                dve.wait_ge(hi_base, KC * (HALVES + h) + c + 1)
                V.scalar_tensor_tensor(H[:, h, c, 1, :], PB[BASE2[h][c]][:], small_col(S_B2 + c), f32(H[:, h, c, 0, :]),
                                       ALU.add, ALU.subtract).then_inc(base_ready, 1)

            def merge(update, dst, n):
                dve.wait_ge(merge_done, n)
                V.scalar_tensor_tensor(dst, update, SCALING, dst, ALU.mult, ALU.add).then_inc(merged, 1)

            def landed(c):
                p0 = P_F2 + 2 * c
                return lambda k: ((p0 + k) % RING, raw_count(p0 + k))

            def merge_pair(n0, which, count):
                for k in range(2):
                    s, n = count(k)
                    dve.wait_ge(raw_in[s], n)
                    merge(MERGE2[k][:, :, which * P:(which + 1) * P],
                          raw[:, s, :].rearrange("p (d n) -> p d n", d=KC), n0 + k)

            def merge_one(n0, count):
                for k in range(2):
                    s, n = count(k)
                    dve.wait_ge(raw_in[s], n)
                    merge(PB[MERGE[k]], raw[:, s, :], n0 + k)

            mask_low(0)
            for c in range(KC):
                base2_lo(0, c)
            mask_low(1)
            merge_one(1, landed(0))
            split_up(P_F2 + 1, 0, lambda k: landed(0)(k)[0])
            su_lo(2)
            for c in range(KC):
                base2_lo(1, c)

            def unit2(c, h):
                ffn_unit(c, h, f2_done, silu2, g_mul2, hi_g2, g_ready2)

            unit2(0, 0)
            merge_pair(3, 0, landed(1))
            split_up(P_F2 + 3, 1, lambda k: landed(1)(k)[0])
            unit2(0, 1)
            merge_pair(3, 1, landed(2))
            split_up(P_F2 + 5, 0, lambda k: landed(2)(k)[0])
            with dve.Fori(0, (C2 - 3) // 2) as i:
                c = 2 * i + 1
                su_lo(i + 3)
                for u in range(2):
                    def count(k, at=landed(3 + u)):
                        return at(k)[0], i * 16 + at(k)[1]
                    unit2(c + u, 0)
                    merge_pair(2 * i + 5, u, count)
                    unit2(c + u, 1)
                    split_up(4 * i + (P_F2 + 6 + 2 * u + 1), (1 + u) % 2, lambda k: count(k)[0])
            for c in range(C2 - 2, C2):
                unit2(c, 0)
                merge_one(C2 + 2 + 2 * (c - C2 + 2), landed(c + 2))
                unit2(c, 1)
                split_up(P_F2 + 2 * (c + 2) + 1, c % 2, lambda k: landed(c + 2)(k)[0])
            for j in range(4, C2):
                p = P_D2 + j
                dve.wait_ge(raw_in[p % RING], raw_count(p))
                merge(PB[j % 2], raw_slot(p), C2 + 1 + j + 1)
                w_lo(p, DOWN2[j])
            for h in range(HALVES):
                for c in range(KC):
                    dve.wait_ge(down2_done, KC * h + c + 1)
                    dve.wait_ge(x1_done, KC * h + c + 1)
                    V.tensor_tensor(X[:, h, c, :], PB[DOWNB[h][c]][:], X[:, h, c, :], ALU.add).then_inc(out_ready, 1)

        @block.tensor
        def _(pe):
            def product(o, w, xx, cols, start, stop):
                pe.matmul(o, w[:, 1, cols], xx[:, 0, :], start=start, stop=False)
                pe.matmul(o, w[:, 0, cols], xx[:, 1, :], start=False, stop=False)
                return pe.matmul(o, w[:, 0, cols], xx[:, 0, :], start=False, stop=stop)

            def chunk(k):
                return slice(k * P, (k + 1) * P)

            def logits(h, k):
                bank, xk = PB[LOGITS[h]], G[:, h, XS + k]
                if k:
                    pe.matmul(bank[0:EXPERTS, :], WR[:, k, 0, :], xk[:, 1, :], start=False, stop=False,
                              skip_group_check=True)
                mm = pe.matmul(bank[0:2 * EXPERTS, :], WR[:, k, :, :].rearrange("p a e -> p (a e)"), xk[:, 0, :],
                               start=(k == 0), stop=(k == KC - 1))
                if k == 0:
                    pe.matmul(bank[0:EXPERTS, :], WR[:, k, 0, :], xk[:, 1, :], start=False, stop=False,
                              skip_group_check=True)
                if k == KC - 1:
                    mm.then_inc(logits_t_done, 1)

            def transpose_logits():
                for h in range(HALVES):
                    pe.wait_ge(logits_copied, HALVES)
                    for t in range(TILES):
                        a = (TILES * h + t) * 2 * EXPERTS
                        mm = pe.transpose(PB[LOGITST][:, a:a + 2 * EXPERTS], LT[:, h, chunk(t)],
                                          sm[0:2 * EXPERTS, S_ID:S_ID + 2 * EXPERTS])
                mm.then_inc(logits_done, 1)

            def low_rank(h, w, bank, ready, count, between=None):
                for k in range(KC):
                    if k == KC - 1 and between:
                        between()
                    pe.wait_ge(ready, count(h, k))
                    mm = product(PB[bank][:], w, G[:, h, XS + k], chunk(k), k == 0, k == KC - 1)
                mm.then_inc(low_done, 1)

            def base(h, banks, ws, p0, frees):
                for k in range(KC):
                    pe.wait_ge(w_ready, p0 + k + 1)
                    for o in range(KC):
                        if k == 0 and frees[o] is not None:
                            pe.wait_ge(*frees[o])
                        product(PB[banks[o]][:], ws[k], G[:, h, XS + k], chunk(o), k == 0, False)

            def add_low(h, banks, w, low, n):
                pe.wait_ge(low_ready, n)
                for o in range(KC):
                    product(PB[banks[o]][:], w, low, chunk(o), False, True).then_inc(base_done, 1)

            def transpose_gates(h):
                pe.wait_ge(gates_done, h + 1)
                for t in range(TILES):
                    mm = pe.transpose(PB[GATEST[h]][:, chunk(t)], T[:, 4 + h, chunk(t)], sm[:, S_ID:S_ID + P])
                mm.then_inc(gates_t_done, 1)

            pe.wait_ge(warm_ready, 1)
            for _ in range(WARM):
                pe.matmul(PB[LOGITS[1]][:], warm[:, 0:P], warm[:], start=True, stop=True)

            def base_0(k, between=None):
                pe.wait_ge(x_ready, x_count(0, k))
                pe.wait_ge(w_ready, P_CW + k + 1)
                for o in range(KC):
                    if o == 2 and between:
                        between()
                    product(PB[BASE1[0][o]], CW[k], G[:, 0, XS + k], chunk(o), k == 0, False)

            base_0(0)
            pe.wait_ge(wr_ready, 1)
            for k in range(KC):
                pe.wait_ge(x_ready, x_count(0, k))
                logits(0, k)
            base_0(1)
            for k in range(KC):
                pe.wait_ge(x_ready, x_count(1, k))
                logits(1, k)
            base_0(2, transpose_logits)
            base_0(3)
            pe.wait_ge(w_ready, P_CA + 1)

            def transpose_both():
                pe.wait_ge(logits_read, 1)
                for h in range(HALVES):
                    transpose_gates(h)

            low_rank(0, CA, LOWB[0], x_ready, x_count, transpose_both)
            low_rank(1, CA, LOWB[1], x_ready, x_count)
            pe.wait_ge(w_ready, P_CB + 1)
            add_low(0, BASE1[0], CB, GATED[0], 1)
            base(1, BASE1[1], CW, P_CW, [(gates_copied, 2), (low_mul, 1), (gates_copied, 1), (base_ready, 1)])

            frees = {0: (base_ready, 3), 1: (base_ready, 4), 2: (low_mul, 2), 3: (base_ready, 2)}
            for h in range(HALVES):
                for k in range(2):
                    pe.wait_ge(w_ready, (P_UP, P_GATE)[k] + 1)
                    pe.wait_ge(*frees[2 * h + k])
                    for c in range(KC):
                        pe.wait_ge(base_ready, KC * h + c + 1)
                        mm = product(PB[(UPB, GATEB)[k][h]][:], (UPW, GATEW)[k], H[:, h, c], chunk(c), c == 0, c == KC - 1)
                    mm.then_inc(upgate_done, 1)
                if h == 0:
                    add_low(1, BASE1[1], CB, GATED[1], 2)

            def ready_count(h, m):
                return 2 * h + m + 1 if m < 2 else 2 * m + h + 1

            for m, h in [(0, 0), (1, 0), (0, 1), (1, 1)] + [(m, h) for m in range(2, ORDERS + 1) for h in range(HALVES)]:
                pe.wait_ge(w_ready, P_AP + m + 1)
                pe.wait_ge(term_ready, ready_count(h, m))
                for o in range(KC):
                    if m == 0 and h == 0:
                        pe.wait_ge(base_ready, KC + o + 1)
                    if m == 0 and h == 1 and o == 0:
                        pe.wait_ge(delta_done, 3)
                        pe.wait_ge(term_mul, 2)
                    mm = product(PB[APB[h][o]][:], APW[m], G[:, h, m], chunk(o), m == 0, m == ORDERS)
                    if m == ORDERS:
                        mm.then_inc(approx_done, 1)
                if m < 4 and h == 1:
                    mm.then_inc(order_done, 1)

            def ffn_unit(c, par, h, done, g_mul, first):
                for k in range(2):
                    if not first:
                        if k == 0:
                            pe.wait_ge(g_mul, 2 * c + h - 1)
                    for d in range(KC):
                        mm = product(PB[PAIR[h][k]][:], WU[:, 2 * par + k], H[:, h, d], chunk(d), d == 0, d == KC - 1)
                    mm.then_inc(done, 1)

            def ffn1_body(c, par, first=False):
                pe.wait_ge(w_ready, 2 * c + (P_F1 + 2))
                for h in range(HALVES):
                    if first:
                        pe.wait_ge(res_added, KC * 0 + 2 * h + 2)
                    ffn_unit(c, par, h, f1_done, g_mul1, first)

            ffn1_body(0, 0, True)
            ffn1_body(1, 1)
            with pe.Fori(0, (C1 - 2) // 2) as i:
                for par in range(2):
                    ffn1_body(2 * i + (2 + par), par)

            def down(h, j, last, slots, p0, done, g_ready, banks):
                pe.wait_ge(w_ready, p0 + j + 1)
                pe.wait_ge(g_ready, 2 * j + h + 1)
                for o in range(KC):
                    mm = product(PB[banks[o]][:], slots[j], G[:, h, j], chunk(o), j == 0, j == last)
                    if j == last:
                        mm.then_inc(done, 1)

            pe.wait_ge(res_added, HALVES * KC)
            for j in range(C1):
                down(0, j, C1 - 1, DOWN1, P_D1, down1_done, g_ready1, DOWNB[0])
            pe.wait_ge(g_mul1, 2 * C1)
            for j in range(C1):
                down(1, j, C1 - 1, DOWN1, P_D1, down1_done, g_ready1, DOWNB[1])

            pe.wait_ge(lora_ready, 1)
            pe.wait_ge(x1_done, 1)
            low_rank(0, A2S, LOW2B[0], x1_ready, lambda h, k: KC * h + k + 1)
            base(0, BASE2[0], W2, P_W2, [(x1_done, 2), (x1_done, 3), (x1_done, 4), (x1_done, KC + 1)])
            pe.wait_ge(lora_ready, 2)
            add_low(0, BASE2[0], B2S, MASKED[0], HALVES + 1)
            pe.wait_ge(x1_done, KC + 2)
            low_rank(1, A2S, LOW2B[1], x1_ready, lambda h, k: KC * h + k + 1)

            def merge_pair(su_n, merged_n):
                pe.wait_ge(su_ready, su_n)
                pe.wait_ge(merged, merged_n)
                for k in range(2):
                    for d in range(KC):
                        mm = pe.matmul(MERGE2[k][:, d, :], S13[:, k, chunk(d)], SU[:, k, :], start=True, stop=True)
                    mm.then_inc(merge_done, 1)

            def merge_down(j, bank):
                pe.matmul(PB[bank][:], S2[:, chunk(j)], S2[:, C2 * P:], start=True, stop=True).then_inc(merge_done, 1)

            pe.wait_ge(stk_ready, 1)
            pe.wait_ge(su_ready, 1)
            for k in range(2):
                pe.wait_ge(base_ready, HALVES * KC + k + 2)
                for d in range(KC):
                    mm = pe.matmul(PB[MERGE[k]][:, chunk(d)], S13[:, k, chunk(d)], SU[:, k, P:], start=True, stop=True)
                mm.then_inc(merge_done, 1)
            base(1, BASE2[1], W2, P_W2, [(x1_done, KC + 3), (x1_done, KC + 4), (low_mul, HALVES + 1), (base_ready, 2 * KC + 1)])
            add_low(1, BASE2[1], B2S, MASKED[1], HALVES + 2)

            for c in range(KC):
                pe.wait_ge(base_ready, HALVES * KC + c + 1)
            pe.wait_ge(low_mul, HALVES + 2)
            pe.wait_ge(w_ready, P_F2 + 2)
            ffn_unit(0, 0, 0, f2_done, g_mul2, True)
            for k in range(2):
                for d in range(KC):
                    pe.wait_ge(base_ready, (HALVES + 1) * KC + d + 1)
                    mm = product(PB[PAIR[1][k]], WU[:, k], H[:, 1, d], chunk(d), d == 0, d == KC - 1)
                mm.then_inc(f2_done, 1)
                if k == 0:
                    merge_pair(2, 2)
            with pe.Fori(0, (C2 - 3) // 2) as i:
                c = 2 * i + 1
                for u in range(2):
                    pe.wait_ge(w_ready, 4 * i + (P_F2 + 2 * (u + 2)))
                    ffn_unit(c + u, (1 + u) % 2, 0, f2_done, g_mul2, False)
                    if u == 0:
                        merge_pair(i + 3, 4 * i + 6)
                    ffn_unit(c + u, (1 + u) % 2, 1, f2_done, g_mul2, False)
            pe.wait_ge(stk_ready, 3)
            for c in range(C2 - 2, C2):
                pe.wait_ge(w_ready, P_F2 + 2 * (c + 1))
                ffn_unit(c, c % 2, 0, f2_done, g_mul2, False)
                for k in range(2):
                    pe.wait_ge(merged, 2 * C2 if c == C2 - 2 else 2 * C2 + k + 1)
                    merge_down(2 * (c - C2 + 2) + k, MERGE[k])
                ffn_unit(c, c % 2, 1, f2_done, g_mul2, False)

            def merge_next(j):
                if j < 6:
                    pe.wait_ge(g_mul2, 2 * C2 - 1)
                else:
                    pe.wait_ge(merged, 2 * C2 + j - 1)
                merge_down(j, j % 2)

            merge_next(4)
            merge_next(5)
            pe.wait_ge(merged, 2 * C2 + 4)
            for j in range(C2):
                if 6 <= j + 4 < C2:
                    merge_next(j + 4)
                down(0, j, C2 - 1, DOWN2, P_D2, down2_done, g_ready2, DOWNB[0])
            pe.wait_ge(g_mul2, 2 * C2)
            for j in range(C2):
                down(1, j, C2 - 1, DOWN2, P_D2, down2_done, g_ready2, DOWNB[1])


def kernel(**inputs):
    import numpy as np
    import concourse.bacc as bacc
    from concourse.bass_utils import run_bass_kernel_spmd

    a = {k: np.asarray(v) for k, v in inputs.items()}

    def by_chunk(w):
        return w.T.reshape(-1, P, w.shape[0]).transpose(1, 0, 2)

    def padded(w, rows):
        return np.concatenate([w, np.zeros((rows - w.shape[0],) + w.shape[1:], w.dtype)])

    xs = a["x"].reshape(HALVES, N, KC, P).transpose(0, 2, 3, 1)
    pieces = list(by_chunk(a["L0_cond_W"]).transpose(1, 0, 2))
    pieces.append(by_chunk(a["L0_cond_A"].reshape(EXPERTS * RANK, D)).reshape(P, D))
    pieces.append(a["L0_cond_B"].transpose(0, 2, 1).reshape(EXPERTS * RANK, D))
    pieces.append(by_chunk(a["L0_attn_up_w"]).reshape(P, D))
    pieces.append(by_chunk(a["L0_attn_gate_w"]).reshape(P, D))
    pieces.append(a["L0_attn_local_approx_output"].T)
    pieces += list(a["L0_attn_fuse_weight"].transpose(2, 1, 0))

    def ffn(gate, up, down, chunks):
        g, u = (by_chunk(padded(w, chunks * P)).reshape(P, KC, chunks, P) for w in (gate, up))
        got = []
        for c in range(chunks):
            got += [g[:, :, c].reshape(P, D), u[:, :, c].reshape(P, D)]
        return got, list(padded(down.T, chunks * P).reshape(chunks, P, D))

    ups1, downs1 = ffn(a["L0_attn_ffn_gate_w"], a["L0_attn_ffn_up_w"], a["L0_attn_ffn_down_w"], C1)
    ups2, downs2 = ffn(a["L0_ffn_w1"], a["L0_ffn_w3"], a["L0_ffn_w2"], C2)
    pieces += ups1 + downs1 + list(by_chunk(a["L0_cond2_W"]).transpose(1, 0, 2)) + ups2 + downs2
    pieces = np.stack(pieces)

    def stacked(w):
        return np.concatenate([padded(w, 32)] * 3)

    b1, b3 = (np.concatenate([np.zeros((KS, P), np.float32), stacked(padded(a[k], C2 * P).T)], axis=1)
              .reshape(KS, (C2 + 1) // 2, 2 * P) for k in ("L0_ffn_lora_B1", "L0_ffn_lora_B3"))
    small = np.concatenate([
        by_chunk(a["L0_cond_Wr"]).reshape(P, KC * EXPERTS),
        a["L0_attn_local_point"].reshape(P, 1),
        a["L0_cond2_b"].reshape(KC, P).T,
        np.broadcast_to(a["L0_attn_discount_factor"], (P, ORDERS)),
        np.broadcast_to((EXPERTS - np.arange(EXPERTS)).astype(np.float32), (P, EXPERTS)),
        np.broadcast_to(np.arange(EXPERTS).astype(np.float32), (P, EXPERTS)),
        np.equal.outer(np.arange(P) // RANK, np.arange(BATCH)).astype(np.float32),
        np.eye(P, dtype=np.float32),
    ], axis=1)
    arrays = {
        "x": xs,
        "ids_b": np.broadcast_to(a["itok_B_0_7"], (P, BATCH)),
        "slot_ids": a["itok_B_0_23"].reshape(1, BATCH),
        "small": small,
        "pieces": pieces,
        "lora_a": a["L0_cond2_lora_As"].reshape(SLOTS, KC, P, RANK).transpose(0, 2, 1, 3).reshape(SLOTS, P, KC * RANK),
        "lora_b": a["L0_cond2_lora_Bs"],
        "stk13": np.stack([stacked(a["L0_ffn_lora_A1"]), stacked(a["L0_ffn_lora_A3"])], axis=1),
        "stk2": np.concatenate([stacked(padded(a["L0_ffn_lora_A2"].T, C2 * P).T), stacked(a["L0_ffn_lora_B2"].T)], axis=1),
        "stk_up": np.stack([b1, b3], axis=2).transpose(1, 0, 2, 3),
    }
    nc = bacc.Bacc("TRN2", target_bir_lowering=False, num_devices=1)
    given, args = {}, []
    for name, v in arrays.items():
        v = np.ascontiguousarray(v)
        given[f"in_{name}"] = v
        args.append(nc.dram_tensor(f"in_{name}", v.shape, mybir.dt.from_np(v.dtype), kind="ExternalInput").ap())
    args.append(nc.dram_tensor("out_x", (HALVES, KC, P, N), F32, kind="ExternalOutput").ap())
    build(nc, *args)
    got = run_bass_kernel_spmd(nc, [given], core_ids=[0]).results[0]["out_x"]
    return got.transpose(0, 3, 1, 2).reshape(BATCH, SEQ, D)
```
